# Optimizing a Trainium2 kernel written in Bass

```python
import numpy as np
import jax
import jax.numpy as jnp

def _softmax(x, axis=-1):
    return jax.nn.softmax(x, axis=axis)

def _gelu(x):
    return jax.nn.gelu(x, approximate=True)

def _silu(x):
    return jax.nn.silu(x)

def _sigmoid(x):
    return jax.nn.sigmoid(x)

def _layernorm(x, axis=-1, eps=1e-05):
    m = jnp.mean(x, axis=axis, keepdims=True)
    v = jnp.var(x, axis=axis, keepdims=True)
    return (x - m) / jnp.sqrt(v + eps)

def _scatter_add(tgt, idx, src, axis=0):
    return tgt.at[idx].add(src)

def _segment_sum(src, seg, n):
    return jax.ops.segment_sum(src, seg, n)
kernel_name = 'mk_perceiver_d1_seqx_r2_d4e591'

def setup_inputs(seed: int=0):
    np.random.seed(seed)
    _w = jnp.asarray

    def _rec_inputs():
        import jax
        import jax.numpy as jnp
        _rk = jax.random.key(seed)
        x = -0.000125 + 0.9999 * jax.random.normal(jax.random.fold_in(_rk, 1), (32, 64, 512), jnp.float32)
        _lenS = 64 - jax.random.randint(jax.random.fold_in(_rk, 7), (32,), 0, max(1, 64 // 4) + 1, jnp.int32)
        _lenS2 = 512 - jax.random.randint(jax.random.fold_in(_rk, 8), (32,), 0, max(1, 512 // 4) + 1, jnp.int32)
        _ctx_1024P = jax.random.normal(jax.random.fold_in(_rk, 11), (32, 16, 512), jnp.float32)
        _ctx_1024c = jax.random.dirichlet(jax.random.fold_in(_rk, 511), 0.3 * jnp.ones((16,), jnp.float32), (32, 512))
        _ctx_1024t = jnp.einsum('bsk,bkd->bsd', _ctx_1024c, _ctx_1024P)
        _ctx_1024t = _ctx_1024t * jax.lax.rsqrt(jnp.mean(jnp.square(_ctx_1024t)) + 1e-12) * 0.953939
        ctx_1024 = -1.52775e-05 + 0.999936 * (_ctx_1024t + 0.3 * jax.random.normal(jax.random.fold_in(_rk, 611), (32, 512, 512), jnp.float32))
        return (x, ctx_1024)
    x, ctx_1024 = _rec_inputs()

    def _L0_xattn_setup():
        import jax, jax.numpy as jnp
        import numpy as np
        B, LP, LQ, H = (16, 1024, 1024, 512)
        key = jax.random.key(seed)
        k1, k2, k3 = jax.random.split(key, 3)
        proj_p = jax.random.normal(k1, (B, LP, H), dtype=jnp.float32)
        proj_q = jax.random.normal(k2, (B, LQ, H), dtype=jnp.float32)
        W = jax.random.normal(k3, (H, H), dtype=jnp.float32) * (1.0 / np.sqrt(H))
        b = jnp.zeros((H,), dtype=jnp.float32)
        return {'proj_p': proj_p, 'proj_q': proj_q, 'W': W, 'b': b}
    _L0_xattn_all = _L0_xattn_setup()
    _L0_xattn_in = {k: v for k, v in _L0_xattn_all.items() if k in ('W', 'b')}
    del _L0_xattn_all

    def _L0_attn_setup():
        import jax, jax.numpy as jnp
        import numpy as np
        DIM = 512
        HEADS = 1
        HDIM = DIM // HEADS
        INNER = 16
        B, L = (2, 2048)
        ROPE_BASE = 32.0

        def _apply_rope(x, pos, base):
            d = x.shape[-1]
            inv_freq = base ** (-jnp.arange(0, d, 2, dtype=jnp.float32) / d)
            ang = pos[:, None].astype(jnp.float32) * inv_freq
            emb = jnp.concatenate([ang, ang], axis=-1)
            cos = jnp.cos(emb)[None, :, None, :].astype(x.dtype)
            sin = jnp.sin(emb)[None, :, None, :].astype(x.dtype)
            x1, x2 = (x[..., :d // 2], x[..., d // 2:])
            rot = jnp.concatenate([-x2, x1], axis=-1)
            return x * cos + rot * sin
        key = jax.random.key(seed)
        ks = jax.random.split(key, 7)
        hidden_states = jax.random.normal(ks[0], (B, L, DIM), dtype=jnp.float32)
        Wq = jax.random.normal(ks[1], (DIM, DIM), dtype=jnp.float32) * 0.02
        Wk = jax.random.normal(ks[2], (DIM, DIM), dtype=jnp.float32) * 0.02
        fc1_w = jax.random.normal(ks[3], (INNER, 1), dtype=jnp.float32) * 0.1
        fc1_b = jax.random.normal(ks[4], (INNER,), dtype=jnp.float32) * 0.1
        fc2_w = jax.random.normal(ks[5], (DIM, INNER), dtype=jnp.float32) * 0.1
        fc2_b = jax.random.normal(ks[6], (DIM,), dtype=jnp.float32) * 0.1
        return {'hidden_states': hidden_states, 'Wq': Wq, 'Wk': Wk, 'fc1_w': fc1_w, 'fc1_b': fc1_b, 'fc2_w': fc2_w, 'fc2_b': fc2_b}
    _L0_attn_all = _L0_attn_setup()
    _L0_attn_in = {k: v for k, v in _L0_attn_all.items() if k in ('Wq', 'Wk', 'fc1_w', 'fc1_b', 'fc2_w', 'fc2_b')}
    del _L0_attn_all

    def _L0_ffn_setup():
        import jax, jax.numpy as jnp
        import numpy as np
        B, S, D, H, E = (8, 1024, 512, 2048, 16)
        key = jax.random.key(seed)
        ks = jax.random.split(key, 4)
        sd = 1.0 / np.sqrt(D).astype(np.float32)
        sh = 1.0 / np.sqrt(H).astype(np.float32)
        return {'x': jax.random.normal(ks[0], (B, S, D), jnp.float32), 'Wg': jax.random.normal(ks[1], (D, E), jnp.float32) * sd, 'bg': jnp.zeros((E,), jnp.float32), 'W1': jax.random.normal(ks[2], (E, D, H), jnp.float32) * sd, 'b1': jnp.zeros((E, H), jnp.float32), 'W2': jax.random.normal(ks[3], (E, H, D), jnp.float32) * sh, 'b2': jnp.zeros((E, D), jnp.float32)}
    _L0_ffn_all = _L0_ffn_setup()
    _L0_ffn_in = {k: v for k, v in _L0_ffn_all.items() if k in ('Wg', 'bg', 'W1', 'b1', 'W2', 'b2')}
    del _L0_ffn_all
    return {'x': x, 'ctx_1024': ctx_1024, 'L0_xattn_W': _L0_xattn_in['W'], 'L0_xattn_b': _L0_xattn_in['b'], 'L0_attn_Wq': _L0_attn_in['Wq'], 'L0_attn_Wk': _L0_attn_in['Wk'], 'L0_attn_fc1_w': _L0_attn_in['fc1_w'], 'L0_attn_fc1_b': _L0_attn_in['fc1_b'], 'L0_attn_fc2_w': _L0_attn_in['fc2_w'], 'L0_attn_fc2_b': _L0_attn_in['fc2_b'], 'L0_ffn_Wg': _L0_ffn_in['Wg'], 'L0_ffn_bg': _L0_ffn_in['bg'], 'L0_ffn_W1': _L0_ffn_in['W1'], 'L0_ffn_b1': _L0_ffn_in['b1'], 'L0_ffn_W2': _L0_ffn_in['W2'], 'L0_ffn_b2': _L0_ffn_in['b2']}

def reference(x, ctx_1024, L0_xattn_W, L0_xattn_b, L0_attn_Wq, L0_attn_Wk, L0_attn_fc1_w, L0_attn_fc1_b, L0_attn_fc2_w, L0_attn_fc2_b, L0_ffn_Wg, L0_ffn_bg, L0_ffn_W1, L0_ffn_b1, L0_ffn_W2, L0_ffn_b2):
    import jax
    import jax.numpy as jnp

    def _L0_xattn_ref(proj_p, proj_q, W, b):
        import jax, jax.numpy as jnp
        import numpy as np
        B, LP, LQ, H = (16, 1024, 1024, 512)
        trans_q = jnp.einsum('bqh,oh->bqo', proj_q, W) + b
        att_weights = jnp.einsum('bph,bqh->bpq', proj_p, trans_q)
        att_norm = jax.nn.softmax(att_weights, axis=-1)
        att_vec = jnp.einsum('bpq,bqh->bph', att_norm, proj_q)
        out = jax.nn.relu(jnp.einsum('bph,oh->bpo', att_vec, W) + b)
        return out

    def _L0_attn_ref(hidden_states, Wq, Wk, fc1_w, fc1_b, fc2_w, fc2_b):
        import jax, jax.numpy as jnp
        import numpy as np
        DIM = 512
        HEADS = 1
        HDIM = DIM // HEADS
        INNER = 16
        B, L = (2, 2048)
        ROPE_BASE = 32.0

        def _apply_rope(x, pos, base):
            d = x.shape[-1]
            inv_freq = base ** (-jnp.arange(0, d, 2, dtype=jnp.float32) / d)
            ang = pos[:, None].astype(jnp.float32) * inv_freq
            emb = jnp.concatenate([ang, ang], axis=-1)
            cos = jnp.cos(emb)[None, :, None, :].astype(x.dtype)
            sin = jnp.sin(emb)[None, :, None, :].astype(x.dtype)
            x1, x2 = (x[..., :d // 2], x[..., d // 2:])
            rot = jnp.concatenate([-x2, x1], axis=-1)
            return x * cos + rot * sin
        b, l, _ = hidden_states.shape
        q = (hidden_states @ Wq.T).reshape(b, l, HEADS, HDIM).astype(jnp.bfloat16)
        k = (hidden_states @ Wk.T).reshape(b, l, HEADS, HDIM).astype(jnp.bfloat16)
        pos = jnp.arange(l)
        q = _apply_rope(q, pos, ROPE_BASE)
        k = _apply_rope(k, pos, ROPE_BASE)
        scores = jnp.einsum('bqhd,bkhd->bhqk', q.astype(jnp.float32), k.astype(jnp.float32)) / HDIM ** 0.5
        causal = jnp.tril(jnp.ones((l, l), dtype=bool))
        exp_qk = jnp.where(causal[None, None], jnp.exp(scores), 0.0)
        o = jnp.swapaxes(exp_qk.sum(axis=-1), 1, 2)
        o = jax.nn.relu(o @ fc1_w.T + fc1_b)
        return o @ fc2_w.T + fc2_b

    def _L0_ffn_ref(x, Wg, bg, W1, b1, W2, b2):
        import jax, jax.numpy as jnp
        import numpy as np
        B, S, D, H, E = (8, 1024, 512, 2048, 16)
        d = x.shape[-1]
        xf = x.reshape(-1, d)
        n_tok = xf.shape[0]
        n_exp = Wg.shape[1]
        cap = -(-n_tok // n_exp)
        score = jax.nn.softmax(xf @ Wg + bg, axis=-1)
        gate = jnp.max(score, axis=-1)
        idx = jnp.argmax(score, axis=-1)
        onehot = jax.nn.one_hot(idx, n_exp, dtype=jnp.int32)
        pos = jnp.sum((jnp.cumsum(onehot, axis=0) - 1) * onehot, axis=-1)
        keep = pos < cap
        safe_pos = jnp.where(keep, pos, cap - 1)
        buf = jnp.zeros((n_exp, cap, d), x.dtype).at[idx, safe_pos].add(jnp.where(keep[:, None], xf, 0.0))
        h = jax.nn.relu(jnp.einsum('ecd,edh->ech', buf, W1) + b1[:, None, :])
        y = jnp.einsum('ech,ehd->ecd', h, W2) + b2[:, None, :]
        out = y[idx, safe_pos] * gate[:, None]
        out = jnp.where(keep[:, None], out, 0.0)
        return out.reshape(x.shape)
    x = x + _L0_xattn_ref(_layernorm(x, axis=-1), ctx_1024, L0_xattn_W, L0_xattn_b)
    x = x + _L0_attn_ref(_layernorm(x, axis=-1), L0_attn_Wq, L0_attn_Wk, L0_attn_fc1_w, L0_attn_fc1_b, L0_attn_fc2_w, L0_attn_fc2_b)
    x = x + _L0_ffn_ref(_layernorm(x, axis=-1), L0_ffn_Wg, L0_ffn_bg, L0_ffn_W1, L0_ffn_b1, L0_ffn_W2, L0_ffn_b2)
    return x

_drawn_inputs = setup_inputs


def setup_inputs(seed=0):
    import zlib

    import numpy as np

    out = dict(_drawn_inputs(seed))
    spreads = {'L0_xattn_b': (0.0, 0.1),
     'L0_ffn_bg': (0.0, 0.298),
     'L0_ffn_b1': (0.0, 0.8),
     'L0_ffn_b2': (0.0, 0.8)}
    factors = {}
    for name, (base, spread) in spreads.items():
        noise = np.random.default_rng([zlib.crc32(name.encode()), seed]).standard_normal(out[name].shape)
        drawn = base * np.exp(spread * noise) if base else spread * noise
        out[name] = jnp.asarray(drawn.astype(out[name].dtype))
    for name, factor in factors.items():
        out[name] = (out[name] * factor).astype(out[name].dtype)
    return out
```

```python
from contextlib import ExitStack

import numpy as np

import concourse.bass as bass
from concourse import mybir

F32 = mybir.dt.float32
F16 = mybir.dt.float16
BF16 = mybir.dt.bfloat16
I32 = mybir.dt.int32
U32 = mybir.dt.uint32
ALU = mybir.AluOpType
ACT = mybir.ActivationFunctionType
AX_X = mybir.AxisListType.X

P = 128
B = 32
L = 64
D = 512
LQ = 512
C = D // P
E = 16
H = 2048
INNER = 16
TOK = B * L
TILES = TOK // P
CAP = -(-TOK // E)
HB = H // D
ROPE_BASE = 32.0
EPS = 1e-5
WS = 64.0
ROW = D + 4
SKIP = 1 << 20
RSQRT_MAGIC = 0x5F3759DF
NEG = -1e30

ORDER = [(1, 0), (1, 1), (2, 0), (1, 2), (1, 3), (2, 1), (2, 2), (2, 3)]
CHUNKS = len(ORDER)
SPLIT_SLOTS = 4
LO_ON_POOL = (1, 4, 6)
HI_ON_DVE = (0, 5)

PB, ST, H1, RT, PX = 0, 128, 256, 384, 400


def program(nc, x, ctx, w_nat, w_t, wq_t, wk_t, b_row, b_col, fc1_w, fc1_b, fc2_t, fc2_b, wg, bg,
            w1, b1, w2, b2, consts, consts16, out):
    with ExitStack() as stack:
        def sb(name, shape, dt):
            return stack.enter_context(nc.sbuf_tensor(name, shape, dt))

        def sem(name):
            return stack.enter_context(nc.semaphore(name))

        def bank(name):
            return stack.enter_context(nc.psum_tensor(name, [P, 512], F32))

        def after(eng, semaphore, count):
            if not isinstance(count, int) or count > 0:
                eng.wait_ge(semaphore, count)

        def alone(eng, semaphore, count):
            after(eng, semaphore, count)
            if not isinstance(count, int):
                eng.sem_inc(passed, 1)

        slot_table = nc.dram_tensor("slot_table", [E * CAP, ROW], F32, kind="Internal").ap()

        raw_low = sb("raw_weights_0_3", [P, 4, 4, D], F32)
        arena = sb("context_then_raw_weights_4_7", [P, 4, 4, D], F32)
        split_arena = sb("raw_projections_then_split_weights", [P, 4, 4, D], F32)
        proj_arena = sb("projections_then_expert_tiles", [P, 4, 4 * D], F32)
        ctx_t = sb("context_transposed", [P, 2, 2, C, LQ], F16)

        raw = [raw_low[:, n] for n in range(4)] + [arena[:, n] for n in range(4)]
        ctx_raw = [arena[:, j] for j in range(2)]
        ctx_nat = [arena[:, 2 + j].rearrange("p c d -> p (c d)").bitcast(F16)
                   .rearrange("p (s c d) -> p s c d", s=2, c=4) for j in range(2)]
        proj_raw = [split_arena[:, n] for n in range(4)]
        w_split = [split_arena[:, n].rearrange("p c d -> p (c d)").bitcast(F16)
                   .rearrange("p (s c d) -> p s c d", s=2, c=4) for n in range(SPLIT_SLOTS)]
        proj = [proj_arena[:, n].bitcast(F16).rearrange("p (s c d) -> p s c d", s=2, c=4) for n in range(4)]
        W_U, W_O, W_Q, W_K = proj

        x_in = sb("x_in", [P, 2, D], F32)
        p_hat = sb("p_hat", [P, D], F32)
        p_t = sb("p_transposed", [P, 2, C, P], F16)
        u_t = sb("u_transposed", [P, 2, C, P], F16)
        probs = sb("probs", [P, LQ], F32)
        probs_t = sb("probs_transposed", [P, 2, C, P], F16)
        att_t = sb("att_transposed", [P, 2, C, P], F16)
        pre = sb("pre_relu", [P, D], F32)
        x1 = sb("x1", [P, 2, D], F32)
        x2_hat = sb("x2_hat", [P, D], F32)
        x2_t = sb("x2_transposed", [P, 2, C, P], F16)
        qk = sb("qk", [P, 2, D], BF16)
        qk_cos = sb("qk_cos", [P, 2, D], BF16)
        qk_sin = sb("qk_sin", [P, 2, D], BF16)
        qk_rot = sb("qk_rotated", [P, 2, D], BF16)
        masked = sb("masked_scores", [P, P], F32)
        exp_t = sb("exp_scores", [P, P], F32)
        inner = sb("inner", [P, P], F32)
        row = sb("rows_for_slots", [P, 2, ROW], F32)
        x3_hat = sb("x3_hat", [P, D], F32)
        x3_t = sb("x3_transposed", [P, 2, C, P], F16)
        fill = sb("empty_slot_row", [P, ROW], F32)

        cst = sb("tables_f32", [P, 2 * P + E + 1], F32)
        ident, mask = cst[:, 0:P], cst[:, P:2 * P]
        desc, p_index = cst[:, 2 * P:2 * P + E], cst[:, 2 * P + E:2 * P + E + 1]
        cst16 = sb("tables_bf16", [P, 2 * D + 2 * P], BF16)
        cos, sin = cst16[:, 0:D], cst16[:, D:2 * D]
        before, ones16 = cst16[:, 2 * D:2 * D + P], cst16[:, 2 * D + P:2 * D + 2 * P]
        b_full = sb("b_on_all_partitions", [P, D], F32)
        b_raw = sb("b_column", [P, C], F32)
        b_split = sb("b_column_split", [P, 2, C], F16)
        fc1_rows = sb("fc1_on_all_rows", [P, P], F32)
        fc1_bias = sb("fc1_bias", [P, 1], F32)
        fc2 = sb("fc2", [P, D], F32)
        wg_raw = sb("wg_raw", [P, C, E], F32)
        wg_split = sb("wg_split", [P, 2, C, E], F16)
        bg_full = sb("bg_on_all_partitions", [P, E], F32)
        b2_raw = sb("b2_raw", [P, D], F32)
        b2_split = sb("b2_split", [P, 2, D], F16)

        stats = sb("stats", [P, 2, 6], F32)
        stats3 = sb("stats3", [P, 6], F32)
        mv = sb("mean_var", [P, 2, 2], F32)
        newton = sb("newton", [P, 3, 3], F32)
        s_max = sb("score_max", [P, 1], F32)
        s_max_b = sb("score_max_with_bias", [P, 1], F32)
        s_shift = sb("score_shift", [P, 1], F32)
        den = sb("denominator", [P, 1], F32)
        rden = sb("reciprocal_denominator", [P, 1], F32)
        logits = sb("logits", [P, E], F32)
        l_max = sb("logit_max", [P, 1], F32)
        l_neg = sb("negative_logit_max", [P, 1], F32)
        l_exp = sb("logit_exp", [P, E], F32)
        l_sum = sb("logit_sum", [P, 1], F32)
        cand = sb("candidates", [P, E], F32)
        rank = sb("rank_of_expert", [P, 1], F32)
        onehot = sb("onehot", [P, E], BF16)
        carry = sb("tokens_so_far", [P, E], BF16)
        px_prod = sb("position_product", [P, E], F32)
        pos = sb("position", [P, 1], F32)
        base = sb("first_slot", [P, 1], F32)
        over = sb("over_capacity", [P, 1], F32)
        slot_f = sb("slot_before_capacity", [P, 1], F32)
        slot = sb("slot", [P, 2, 1], I32)
        token = sb("token", [P, 1], F32)

        ffn = proj_arena[:, :].rearrange("p a b -> p (a b)")
        taken = [0]

        def carve(n):
            at = taken[0]
            taken[0] = at + n
            assert taken[0] <= 16 * D
            return ffn[:, at:at + n]

        e_row = [carve(ROW) for _ in range(2)]
        e_hat = carve(D)
        e_t = carve(D).bitcast(F16).rearrange("p (s c n) -> p s c n", s=2, c=C)
        hid = [carve(D) for _ in range(2)]
        hid_split = [carve(D).bitcast(F16).rearrange("p (s n) -> p s n", s=2) for _ in range(HB)]
        o_row = [carve(D) for _ in range(2)]
        b1_e = [carve(H // P) for _ in range(2)]
        gate_e = [carve(1) for _ in range(2)]
        sel = carve(P // 2).bitcast(F16)
        is_e = carve(1)
        e_index = carve(1)

        scores_ps = bank("scores_ps")
        ctx_ps = [bank("ctx_ps0"), bank("ctx_ps1")]
        tr_ps = bank("transposes_ps")
        ua_ps = bank("u_q_att_ps")
        of_ps = bank("out_fc2_ps")
        k_ps = bank("k_ps")
        small_ps = bank("small_ps")
        hid_ps = [ctx_ps[0], ctx_ps[1]]
        y_ps = of_ps

        passed = sem("waits_passed")
        consts_in = sem("consts_in")
        proj_in = [sem(f"proj_in{n}") for n in range(4)]
        proj_hi = sem("proj_hi")
        proj_lo = sem("proj_lo")
        small_hi = sem("small_hi")
        small_lo = sem("small_lo")
        zeroed = sem("zeroed")
        padded = sem("padded")
        filled = sem("table_filled")
        x_loaded = [sem(f"x_loaded{n}") for n in range(2)]
        ctx_loaded = [sem(f"ctx_loaded{n}") for n in range(2)]
        ln_stats = [sem(f"ln{n}_stats") for n in range(3)]
        ln_mv = [sem(f"ln{n}_mean_var") for n in range(3)]
        ln_step = [sem(f"ln{n}_rsqrt_steps") for n in range(3)]
        ln_hat = [sem(f"ln{n}_normalised") for n in range(3)]
        p_tr = sem("p_transposes")
        p_hi = sem("p_hi")
        p_lo = sem("p_lo")
        u_done = sem("u_done")
        u_hi = sem("u_hi")
        u_lo = sem("u_lo")
        pb_done = sem("pb_done")
        ctx_tr = sem("ctx_transpose_groups")
        ctx_hi = sem("ctx_t_hi_groups")
        ctx_lo = sem("ctx_t_lo_groups")
        nat_hi = sem("ctx_natural_hi_batches")
        nat_lo = sem("ctx_natural_lo_batches")
        s_done = sem("scores_done")
        s_maxed = sem("scores_maxed")
        s_biased = sem("scores_max_biased")
        s_shifted = sem("scores_shift")
        p_exp = sem("probs_exp")
        rden_ready = sem("rden_ready")
        rden_scaled = sem("rden_scaled")
        pt_tr = sem("probs_transposes")
        pt_hi = sem("probs_hi")
        pt_lo = sem("probs_lo")
        att_done = sem("att_done")
        att_hi = sem("att_hi")
        att_lo = sem("att_lo")
        out_done = sem("out_done")
        pre_done = sem("pre_relu_done")
        x1_done = sem("x1_done")
        x2_tr = sem("x2_transposes")
        x2_hi = sem("x2_hi")
        x2_lo = sem("x2_lo")
        q_done = sem("q_done")
        k_done = sem("k_done")
        q_cast = sem("q_cast")
        k_cast = sem("k_cast")
        rope_parts = sem("rope_parts")
        roped = sem("roped")
        st_done = sem("st_done")
        masked_done = sem("masked_done")
        exp_done = sem("exp_done")
        h1_done = sem("h1_done")
        inner_done = sem("inner_done")
        fc2_done = sem("fc2_done")
        x2_done = sem("x2_done")
        x3_tr = sem("x3_transposes")
        x3_hi = sem("x3_hi")
        x3_lo = sem("x3_lo")
        logits_mm = sem("logits_mm")
        logits_done = sem("logits_done")
        l_maxed = sem("logits_maxed")
        l_negated = sem("logits_max_negated")
        l_exped = sem("logits_exp")
        cand_done = sem("candidates_done")
        rank_done = sem("rank_done")
        onehot_done = sem("onehot_done")
        px_done = sem("prefix_done")
        carry_done = sem("carry_done")
        pos_done = sem("position_done")
        base_done = sem("first_slot_done")
        over_done = sem("over_done")
        slot_f_done = sem("slot_f_done")
        row_ready = sem("row_ready")
        token_written = sem("token_written")
        token_next = sem("token_next")
        base_out = [sem(f"x2_stored{n}") for n in range(2)]
        scattered = [sem(f"row_scattered{n}") for n in range(2)]

        w_in = [sem(f"w_chunk_loaded{n}") for n in range(CHUNKS)]
        w_scaled = [sem(f"w_chunk_scaled{n}") for n in range(CHUNKS)]
        w_hi = [sem(f"w_chunk_hi{n}") for n in range(CHUNKS)]
        w_lo = [sem(f"w_chunk_lo{n}") for n in range(CHUNKS)]
        w_used = sem("w_chunks_used")
        e_loaded = [sem(f"expert_rows_loaded{n}") for n in range(2)]
        b1_loaded = [sem(f"b1_loaded{n}") for n in range(2)]
        e_norm = sem("expert_rows_normalised")
        e_tr = sem("expert_transposes")
        e_hi = sem("expert_rows_hi")
        e_lo = sem("expert_rows_lo")
        e_idx = sem("expert_index")
        e_sel = sem("expert_selected")
        e_sel_steps = sem("expert_select_steps")
        gate_done = sem("gate_done")
        h_relu = sem("hidden_blocks_relu")
        h_hi = sem("hidden_blocks_hi")
        h_lo = sem("hidden_blocks_lo")
        y_out = sem("y_out")
        out_scat = [sem(f"out_scattered{n}") for n in range(2)]

        block = stack.enter_context(nc.Block())

        def each_step(eng, step):
            for i in range(-1, 4):
                step(i, i // 2, i % 2, ahead=True, cur=i >= 0, back1=i >= 1, back2=i >= 2)
            with eng.Fori(2, TILES // 2 - 1) as k:
                for p in range(2):
                    step(2 * k + p, k, p, ahead=True, cur=True, back1=True, back2=True)
            for i in range(TILES - 2, TILES + 2):
                step(i, i // 2, i % 2, ahead=i < TILES - 1, cur=i < TILES, back1=i <= TILES, back2=True)

        def each_expert(eng, expert):
            for p in range(2):
                expert(p, 0, p, False)
            with eng.Fori(1, E // 2 - 1) as k:
                for p in range(2):
                    expert(2 * k + p, k, p, False)
            for p in range(2):
                expert(E - 2 + p, E // 2 - 1, p, p == 1)

        def neighbour(k, p, d):
            return k + (p + d) // 2, (p + d) % 2

        w1_chunks = w1.rearrange("e (c p) h -> e p c h", p=P)
        w2_chunks = w2.rearrange("e (m c p) d -> e m p c d", p=P, c=4)

        def chunk_source(e, kk):
            which, hb = ORDER[kk]
            if which == 1:
                return w1_chunks[bass.ds(e, 1), :, :, hb * D:(hb + 1) * D].rearrange("o p c h -> (o p) c h")
            return w2_chunks[bass.ds(e, 1), hb].rearrange("o p c d -> (o p) c d")

        @block.sync
        def _(sp):
            sp.dma_start(cst[:], consts).then_inc(consts_in, 16)
            sp.dma_start(x_in[:, 0], x[0:P, :]).then_inc(x_loaded[0], 16)
            for n, w in enumerate((w_nat, w_t, wq_t, wk_t)):
                sp.dma_start(proj_raw[n], w.rearrange("(c p) d -> p c d", p=P)).then_inc(proj_in[n], 16)
                if n < 2:
                    sp.dma_start(ctx_raw[n], ctx[n].rearrange("(p c) d -> p c d", c=4)).then_inc(ctx_loaded[n], 16)
            sp.dma_start(cst16[:], consts16).then_inc(consts_in, 16)
            sp.dma_start(b_full[:], b_row.partition_broadcast(P)).then_inc(consts_in, 16)
            sp.dma_start(b_raw[:], b_col).then_inc(consts_in, 16)
            sp.dma_start(bg_full[:], bg.partition_broadcast(P)).then_inc(consts_in, 16)
            sp.dma_start(wg_raw[:], wg.rearrange("(c p) e -> p c e", p=P)).then_inc(consts_in, 16)
            alone(sp, zeroed, 4)
            sp.dma_start(fc1_rows[:, 0:INNER], fc1_w.partition_broadcast(P)).then_inc(padded, 16)
            sp.dma_start(fc1_bias[0:INNER, :], fc1_b).then_inc(padded, 16)
            sp.dma_start(fc2[0:INNER, :], fc2_t).then_inc(padded, 16)
            sp.dma_start(fc2[32:33, :], fc2_b).then_inc(padded, 16)
            sp.dma_start(b2_raw[0:E, :], b2).then_inc(padded, 16)
            alone(sp, filled, 1)
            for n in range(E * CAP // P):
                sp.dma_start(slot_table[n * P:(n + 1) * P, :], fill[:]).then_inc(filled, 16)
            for kk in range(4):
                sp.dma_start(raw[kk], chunk_source(0, kk)).then_inc(w_in[kk], 16)

            def step(i, k, p, ahead, cur, back1, back2):
                if isinstance(i, int) and i + 2 >= TILES:
                    return
                if isinstance(i, int) and i == -1:
                    sp.dma_start(x_in[:, 1], x[P:2 * P, :]).then_inc(x_loaded[1], 16)
                    t = 1
                else:
                    t = i + 2
                    alone(sp, x1_done, t - 1)
                    sp.dma_start(x_in[:, p], x[bass.ds(t * P, P), :]).then_inc(x_loaded[p], 16)
                for j in range(2):
                    alone(sp, ctx_tr, 8 * (t - 1) + 4 * j + 4)
                    alone(sp, nat_lo, 2 * (t - 1) + j + 1)
                    sp.dma_start(ctx_raw[j], ctx[bass.ds(2 * t + j, 1)].rearrange("o (p c) d -> (o p) c d", c=4)
                                 ).then_inc(ctx_loaded[j], 16)

            each_step(sp, step)

            def load_rows(e, k, p):
                alone(sp, out_scat[p], 16 * k)
                sp.dma_start(e_row[p], slot_table[bass.ds(e * CAP, CAP), :]).then_inc(e_loaded[p], 16)
                sp.dma_start(b1_e[p], b1[bass.ds(e, 1)].rearrange("o p c -> (o p) c")).then_inc(b1_loaded[p], 16)

            def load_expert(e, k, p):
                for kk in range(CHUNKS):
                    alone(sp, w_lo[kk], e)
                    sp.dma_start(raw[kk], chunk_source(e, kk)).then_inc(w_in[kk], 16)
                    if kk == 3:
                        load_rows(e, k, p)

            for kk in range(4, CHUNKS):
                alone(sp, att_done, TILES)
                sp.dma_start(raw[kk], chunk_source(0, kk)).then_inc(w_in[kk], 16)
            for n in range(2):
                alone(sp, scattered[n], 16 * (TILES // 2))
            alone(sp, k_done, TILES)
            load_rows(0, 0, 0)
            load_expert(1, 0, 1)
            with sp.Fori(1, E // 2) as k:
                for p in range(2):
                    load_expert(2 * k + p, k, p)

        @block.tensor
        def _(pe):
            def three(out_ps, left, right, first, last):
                pe.matmul(out_ps, left[0], right[0], start=first, stop=False)
                pe.matmul(out_ps, left[0], right[1], start=False, stop=False)
                return pe.matmul(out_ps, left[1], right[0], start=False, stop=last)

            def both(a, *at):
                return (a[(slice(None), 0) + at], a[(slice(None), 1) + at])

            def transpose4(source):
                for c in range(C):
                    mm = pe.transpose(tr_ps[:, c * P:(c + 1) * P], source[:, c * P:(c + 1) * P], ident)
                return mm

            def cols(c):
                return slice(c * P, (c + 1) * P)

            A = slice(None)

            def ctx_group(t, g):
                j, hc = g // 4, g % 4
                if g % 4 == 0:
                    pe.wait_ge(ctx_loaded[j], 16 * (t + 1))
                after(pe, ctx_lo, 8 * t + g - 1)
                for c in range(C):
                    mm = pe.transpose(ctx_ps[g % 2][:, cols(c)], ctx_raw[j][:, c, cols(hc)], ident)
                mm.then_inc(ctx_tr, 1)

            def step(i, k, p, ahead, cur, back1, back2):
                if cur:
                    pe.wait_ge(u_lo, i + 1)
                    pe.wait_ge(ctx_lo, 8 * (i + 1))
                    after(pe, p_exp, i)
                    for c in range(C):
                        for n, (a, b) in enumerate(((0, 0), (0, 1), (1, 0))):
                            for j in range(2):
                                mm = pe.matmul(scores_ps[j * L:(j + 1) * L, :], u_t[:, a, c, j * L:(j + 1) * L],
                                               ctx_t[:, j, b, c, :], start=(c == 0 and n == 0),
                                               stop=(c == C - 1 and n == 2))
                    mm.then_inc(s_done, 1)
                for oc in range(2 * C):
                    if back1:
                        w, ps = (W_Q, ua_ps) if oc < C else (W_K, k_ps)
                        if oc == 0:
                            pe.wait_ge(x2_lo, i)
                            after(pe, u_lo, i + 1 if cur else i)
                        if oc == C:
                            after(pe, k_cast, i - 1)
                        for c in range(C):
                            mm = three(ps[:, cols(oc % C)], both(w, c, cols(oc % C)), both(x2_t, c, A), c == 0, c == C - 1)
                        if oc == C - 1:
                            mm.then_inc(q_done, 1)
                        if oc == 2 * C - 1:
                            mm.then_inc(k_done, 1)
                    if ahead:
                        ctx_group(i + 1, oc)
                    if oc == 1 and back2:
                        pe.wait_ge(ln_hat[2], i - 1)
                        pe.wait_ge(x2_lo, i if back1 else TILES)
                        transpose4(x3_hat).then_inc(x3_tr, 1)
                    if oc == 3 and cur:
                        pe.wait_ge(p_exp, i + 1)
                        if back2:
                            pe.wait_ge(x3_lo, i - 1)
                        elif back1:
                            pe.wait_ge(x2_lo, i)
                        after(pe, p_lo, i + 1)
                        transpose4(probs).then_inc(pt_tr, 1)
                    if oc == 4 and back2:
                        pe.wait_ge(x3_lo, i - 1)
                        if cur:
                            pe.wait_ge(s_shifted, i + 1)
                        else:
                            pe.wait_ge(inner_done, i - 1)
                        for c in range(C):
                            mm = three(small_ps[:, RT:RT + E], both(x3_t, c, A), both(wg_split, c, A), c == 0, c == C - 1)
                        mm.then_inc(logits_mm, 1)
                    if oc == 6 and back2:
                        pe.wait_ge(onehot_done, i - 1)
                        pe.wait_ge(carry_done, i - 1)
                        pe.matmul(small_ps[:, PX:PX + E], before, onehot[:], start=True, stop=False)
                        pe.matmul(small_ps[:, PX:PX + E], ones16, carry[:], start=False, stop=True).then_inc(px_done, 1)
                if cur:
                    pe.wait_ge(pt_lo, i + 1)
                    pe.wait_ge(nat_lo, 2 * i + 2)
                    if back1:
                        pe.wait_ge(q_cast, i)
                    after(pe, u_lo, i + 1)
                    for j in range(2):
                        for hc in range(C):
                            for c in range(C):
                                mm = three(ua_ps[:, hc * P + j * L:hc * P + (j + 1) * L],
                                           both(ctx_nat[j], c, cols(hc)), both(probs_t, c, slice(j * L, (j + 1) * L)),
                                           c == 0, c == C - 1)
                    mm.then_inc(att_done, 1)
                if ahead:
                    pe.wait_ge(ln_hat[0], i + 2)
                    after(pe, pt_lo, i + 1)
                    if isinstance(i, int) and i == -1:
                        pe.wait_ge(consts_in, 16 * 6)
                    transpose4(p_hat).then_inc(p_tr, 1)
                if back1:
                    pe.wait_ge(roped, i)
                    if back2:
                        pe.wait_ge(pos_done, i - 1)
                    else:
                        pe.wait_ge(s_shifted, i + 1)
                    for c in range(C):
                        mm = pe.matmul(small_ps[:, ST:ST + P], qk_rot[:, 1, cols(c)], qk_rot[:, 0, cols(c)],
                                       start=(c == 0), stop=(c == C - 1))
                    mm.then_inc(st_done, 1)
                if cur:
                    pe.wait_ge(att_lo, i + 1)
                    after(pe, x2_done, i - 1)
                    for c in range(C):
                        mm = three(of_ps[:, :], both(att_t, c, A), both(W_O, c, A), c == 0, c == C - 1)
                    mm.then_inc(out_done, 1)
                if back1:
                    pe.wait_ge(exp_done, i)
                    if isinstance(i, int) and i == 1:
                        pe.wait_ge(padded, 16 * 5)
                    pe.matmul(small_ps[:, H1:H1 + P], fc1_rows[:], exp_t[:], start=True, stop=True).then_inc(h1_done, 1)
                if ahead:
                    pe.wait_ge(p_lo, i + 2)
                    after(pe, att_lo, i + 1)
                    if back1:
                        pe.wait_ge(inner_done, i)
                    else:
                        after(pe, s_shifted, i + 1)
                    if isinstance(i, int) and i == -1:
                        pe.wait_ge(proj_lo, 1)
                        pe.wait_ge(small_lo, 1)
                    for hc in range(C):
                        for c in range(C):
                            mm = three(ua_ps[:, cols(hc)], both(W_U, c, cols(hc)), both(p_t, c, A), c == 0, c == C - 1)
                    mm.then_inc(u_done, 1)
                    for c in range(C):
                        mm = three(small_ps[:, PB:PB + 1], both(p_t, c, A), both(b_split, slice(c, c + 1)),
                                   c == 0, c == C - 1)
                    mm.then_inc(pb_done, 1)
                    if isinstance(i, int) and i == -1:
                        pe.wait_ge(proj_lo, 4)
                if back1:
                    pe.wait_ge(inner_done, i)
                    if cur:
                        pe.wait_ge(pre_done, i + 1)
                    else:
                        pe.wait_ge(x2_done, i - 1)
                    pe.matmul(of_ps[:, :], inner[:], fc2[:], start=True, stop=True).then_inc(fc2_done, 1)
                if cur:
                    pe.wait_ge(ln_hat[1], i + 1)
                    if ahead:
                        pe.wait_ge(p_lo, i + 2)
                    transpose4(x2_hat).then_inc(x2_tr, 1)

            pe.wait_ge(consts_in, 16 * 6)
            each_step(pe, step)

            def transpose_rows(e):
                pe.wait_ge(e_norm, e + 1)
                transpose4(e_hat).then_inc(e_tr, 1)

            def expert(e, k, p, last):
                for kk, (which, hb) in enumerate(ORDER):
                    w = w_split[kk % SPLIT_SLOTS]
                    pe.wait_ge(w_lo[kk], e + 1)
                    if which == 1:
                        if kk == 0:
                            pe.wait_ge(e_lo, e + 1)
                        n = 4 * e + hb
                        after(pe, h_relu, n - 1)
                        for hc in range(C):
                            for c in range(C):
                                mm = three(hid_ps[hb % 2][:, cols(hc)], both(w, c, cols(hc)), both(e_t, c, A),
                                           c == 0, c == C - 1)
                        mm.then_inc(w_used, 1)
                    else:
                        pe.wait_ge(h_lo, 4 * e + hb + 1)
                        if hb == 0:
                            after(pe, y_out, e)
                            pe.wait_ge(e_sel, e + 1)
                            pe.matmul(y_ps[:, :], sel, b2_split[:, 0], start=True, stop=False)
                            pe.matmul(y_ps[:, :], sel, b2_split[:, 1], start=False, stop=False)
                        for c in range(C):
                            mm = three(y_ps[:, :], both(hid_split[hb], cols(c)), both(w, c, A),
                                       False, hb == HB - 1 and c == C - 1)
                        mm.then_inc(w_used, 1)
                    if kk == 5 and not last:
                        transpose_rows(e + 1)

            transpose_rows(0)
            each_expert(pe, expert)

        @block.scalar
        def _(act):
            def hi(dst, src, produced, count, done, scale=1.0):
                act.wait_ge(produced, count)
                act.activation(dst, src, ACT.Copy, scale=scale).then_inc(done, 1)

            def flat(a, s):
                return a[:, s].rearrange("p c n -> p (c n)")

            act.wait_ge(consts_in, 16 * 6)
            for n in range(4):
                hi(proj[n][:, 0], proj_raw[n], proj_in[n], 16, proj_hi, scale=WS)
                if n == 0:
                    act.activation(b_split[:, 0], b_raw[:], ACT.Copy, scale=WS).then_inc(small_hi, 1)
                    act.activation(wg_split[:, 0], wg_raw[:], ACT.Copy, scale=WS).then_inc(small_hi, 1)
            act.wait_ge(padded, 16 * 5)
            act.activation(b2_split[:, 0], b2_raw[:], ACT.Copy, scale=WS).then_inc(small_hi, 1)

            def step(i, k, p, ahead, cur, back1, back2):
                if back1:
                    hi(flat(x2_t, 0), tr_ps[:, :], x2_tr, i, x2_hi)
                if cur:
                    act.wait_ge(s_shifted, i + 1)
                    after(act, pt_tr, i)
                    act.activation(probs[:], scores_ps[:, :], ACT.Exp, bias=s_shift[:], scale=1.0,
                                   accum_out=den[:]).then_inc(p_exp, 1)
                for g in range(8):
                    if ahead:
                        hi(ctx_t[:, g // 4, 0, g % 4, :], ctx_ps[g % 2][:, :], ctx_tr, 8 * (i + 1) + g + 1, ctx_hi)
                    if g == 1 and back2:
                        hi(flat(x3_t, 0), tr_ps[:, :], x3_tr, i - 1, x3_hi)
                    if g == 3 and cur:
                        hi(flat(probs_t, 0), tr_ps[:, :], pt_tr, i + 1, pt_hi)
                    if g == 3 and back1:
                        after(act, rope_parts, 3 * (i - 1))
                        hi(qk[:, 0, :], ua_ps[:, :], q_done, i, q_cast, scale=1.0 / WS)
                    if g == 6 and back2:
                        act.wait_ge(l_negated, i - 1)
                        after(act, row_ready, i - 2)
                        act.activation(l_exp[:], logits[:], ACT.Exp, bias=l_neg[:], scale=1.0,
                                       accum_out=l_sum[:]).then_inc(l_exped, 1)
                if back1:
                    hi(qk[:, 1, :], k_ps[:, :], k_done, i, k_cast, scale=1.0 / WS)
                if cur:
                    hi(flat(att_t, 0), ua_ps[:, :], att_done, i + 1, att_hi)
                if ahead:
                    hi(flat(p_t, 0), tr_ps[:, :], p_tr, i + 2, p_hi)
                    for j in range(2):
                        act.wait_ge(ctx_loaded[j], 16 * (i + 2))
                        act.activation(ctx_nat[j][:, 0], ctx_raw[j], ACT.Copy).then_inc(nat_hi, 1)
                        if j == 0 and back1:
                            act.wait_ge(masked_done, i)
                            after(act, h1_done, i - 1)
                            act.activation(exp_t[:], masked[:], ACT.Exp).then_inc(exp_done, 1)
                elif back1:
                    act.wait_ge(masked_done, i)
                    act.wait_ge(h1_done, i - 1)
                    act.activation(exp_t[:], masked[:], ACT.Exp).then_inc(exp_done, 1)
                if back1:
                    act.wait_ge(h1_done, i)
                    after(act, fc2_done, i - 1)
                    if isinstance(i, int) and i == 1:
                        act.wait_ge(zeroed, 5)
                    act.activation(inner[:], small_ps[:, H1:H1 + P], ACT.Relu, bias=fc1_bias[:]).then_inc(inner_done, 1)
                if ahead:
                    hi(flat(u_t, 0), ua_ps[:, :], u_done, i + 2, u_hi, scale=1.0 / WS)

            each_step(act, step)

            def rows_hi(e):
                hi(flat(e_t, 0), tr_ps[:, :], e_tr, e + 1, e_hi)

            def expert(e, k, p, last):
                for kk, (which, hb) in enumerate(ORDER):
                    if kk not in HI_ON_DVE:
                        if kk in LO_ON_POOL:
                            act.wait_ge(w_scaled[kk], e + 1)
                        else:
                            act.wait_ge(w_in[kk], 16 * (e + 1))
                        after(act, w_used, 8 * e + kk - SPLIT_SLOTS + 1)
                        act.activation(w_split[kk % SPLIT_SLOTS][:, 0], raw[kk], ACT.Copy,
                                       scale=1.0 if kk in LO_ON_POOL else WS).then_inc(w_hi[kk], 1)
                    for hb in {2: (0,), 3: (1,), 5: (2,), 6: (3,)}.get(kk, ()):
                        act.wait_ge(w_used, CHUNKS * e + ORDER.index((1, hb)) + 1)
                        after(act, h_lo, 4 * e + hb - 1)
                        if hb == 0:
                            act.wait_ge(b1_loaded[p], 16 * (k + 1))
                        for hc in range(C):
                            r = act.activation(hid[hb % 2][:, hc * P:(hc + 1) * P],
                                               hid_ps[hb % 2][:, hc * P:(hc + 1) * P], ACT.Relu,
                                               bias=b1_e[p][:, 4 * hb + hc:4 * hb + hc + 1], scale=1.0 / WS)
                        r.then_inc(h_relu, 1)
                    if kk == 7 and not last:
                        rows_hi(e + 1)

            rows_hi(0)
            each_expert(act, expert)

        @block.vector
        def _(dve):
            def lo(dst, src, high, done_hi, count, done, scale=1.0):
                dve.wait_ge(done_hi, count)
                if scale == 1.0:
                    dve.tensor_tensor(dst, src, high, ALU.subtract).then_inc(done, 1)
                else:
                    dve.scalar_tensor_tensor(out=dst, in0=src, scalar=scale, in1=high, op0=ALU.mult,
                                             op1=ALU.subtract).then_inc(done, 1)

            def flat(a, s):
                return a[:, s].rearrange("p c n -> p (c n)")

            def norm_stats(n, t, source, st, moments):
                dve.bn_stats(st, source).then_inc(ln_stats[n], 1)
                alone(dve, ln_stats[n], t + 1)
                dve.bn_aggr(moments, st).then_inc(ln_mv[n], 1)

            dve.memset(fc1_rows[:], 0.0).then_inc(zeroed, 1)
            dve.memset(fc1_bias[:], 0.0).then_inc(zeroed, 1)
            dve.memset(fc2[:], 0.0).then_inc(zeroed, 1)
            dve.memset(b2_raw[:], 0.0).then_inc(zeroed, 1)
            dve.memset(carry[:], 0.0).then_inc(carry_done, 1)
            dve.wait_ge(zeroed, 4)
            dve.memset(fc1_bias[32:33, :], 1.0).then_inc(zeroed, 1)
            dve.wait_ge(consts_in, 16 * 6)
            dve.tensor_copy(token[:], p_index).then_inc(token_next, 1)
            dve.wait_ge(x_loaded[0], 16)
            norm_stats(0, 0, x_in[:, 0], stats[:, 0], mv[:, 0])
            for n in range(4):
                dve.wait_ge(proj_hi, n + 1)
                dve.scalar_tensor_tensor(out=proj[n][:, 1], in0=proj_raw[n], scalar=WS, in1=proj[n][:, 0],
                                         op0=ALU.mult, op1=ALU.subtract).then_inc(proj_lo, 1)
                if n == 0:
                    dve.wait_ge(small_hi, 2)
                    dve.scalar_tensor_tensor(out=b_split[:, 1], in0=b_raw[:], scalar=WS, in1=b_split[:, 0],
                                             op0=ALU.mult, op1=ALU.subtract)
                    dve.scalar_tensor_tensor(out=wg_split[:, 1], in0=wg_raw[:], scalar=WS, in1=wg_split[:, 0],
                                             op0=ALU.mult, op1=ALU.subtract).then_inc(small_lo, 1)
            dve.wait_ge(small_hi, 3)
            dve.scalar_tensor_tensor(out=b2_split[:, 1], in0=b2_raw[:], scalar=WS, in1=b2_split[:, 0],
                                     op0=ALU.mult, op1=ALU.subtract).then_inc(small_lo, 1)

            def step(i, k, p, ahead, cur, back1, back2):
                ka, pa = neighbour(k, p, 1)
                k1, p1 = neighbour(k, p, -1)
                if back1:
                    lo(flat(x2_t, 1), tr_ps[:, :], flat(x2_t, 0), x2_hi, i, x2_lo)
                if cur:
                    dve.wait_ge(s_done, i + 1)
                    dve.reduce_max(s_max[:], scores_ps[:, :], AX_X).then_inc(s_maxed, 1)
                if back2:
                    dve.wait_ge(fc2_done, i - 1)
                    after(dve, scattered[p], 16 * (k - 1))
                    after(dve, base_out[p], 16 * (k - 1))
                    dve.tensor_tensor(row[:, p, 0:D], of_ps[:, :], x1[:, p], ALU.add).then_inc(x2_done, 1)
                if cur:
                    dve.wait_ge(s_maxed, i + 1)
                    dve.wait_ge(pb_done, i + 1)
                    dve.scalar_tensor_tensor(out=s_max_b[:], in0=small_ps[:, PB:PB + 1], scalar=1.0 / WS,
                                             in1=s_max[:], op0=ALU.mult, op1=ALU.add).then_inc(s_biased, 1)
                    dve.wait_ge(s_biased, i + 1)
                    after(dve, p_exp, i)
                    dve.scalar_tensor_tensor(out=s_shift[:], in0=small_ps[:, PB:PB + 1], scalar=1.0 / WS,
                                             in1=s_max_b[:], op0=ALU.mult, op1=ALU.subtract).then_inc(s_shifted, 1)
                if back2:
                    dve.wait_ge(x2_done, i - 1)
                    norm_stats(2, i - 2, row[:, p, 0:D], stats3[:], row[:, p, D:D + 2])
                for g in range(8):
                    if ahead:
                        lo(ctx_t[:, g // 4, 1, g % 4, :], ctx_ps[g % 2][:, :], ctx_t[:, g // 4, 0, g % 4, :],
                           ctx_hi, 8 * (i + 1) + g + 1, ctx_lo)
                    if g == 0 and ahead and not (isinstance(i, int) and i == -1):
                        dve.wait_ge(x_loaded[pa], 16 * (ka + 1))
                        after(dve, ln_hat[0], i + 1)
                        norm_stats(0, i + 1, x_in[:, pa], stats[:, 0], mv[:, 0])
                    if g == 1 and back2:
                        lo(flat(x3_t, 1), tr_ps[:, :], flat(x3_t, 0), x3_hi, i - 1, x3_lo)
                    if g == 3 and cur:
                        lo(flat(probs_t, 1), tr_ps[:, :], flat(probs_t, 0), pt_hi, i + 1, pt_lo)
                        dve.wait_ge(p_exp, i + 1)
                        dve.reciprocal(rden[:], den[:]).then_inc(rden_ready, 1)
                        dve.wait_ge(rden_ready, i + 1)
                        dve.tensor_scalar(rden[:], rden[:], 1.0 / WS, None, ALU.mult).then_inc(rden_scaled, 1)
                    if g == 4 and back2:
                        dve.wait_ge(logits_mm, i - 1)
                        dve.scalar_tensor_tensor(out=logits[:], in0=small_ps[:, RT:RT + E], scalar=1.0 / WS,
                                                 in1=bg_full[:], op0=ALU.mult, op1=ALU.add).then_inc(logits_done, 1)
                        dve.wait_ge(logits_done, i - 1)
                        dve.reduce_max(l_max[:], logits[:], AX_X).then_inc(l_maxed, 1)
                        dve.wait_ge(l_maxed, i - 1)
                        dve.tensor_scalar(l_neg[:], l_max[:], -1.0, None, ALU.mult).then_inc(l_negated, 1)
                        dve.scalar_tensor_tensor(out=cand[:], in0=logits[:], scalar=l_max[:, 0:1], in1=desc,
                                                 op0=ALU.is_equal, op1=ALU.mult).then_inc(cand_done, 1)
                    if g == 5 and back2:
                        dve.wait_ge(cand_done, i - 1)
                        dve.reduce_max(rank[:], cand[:], AX_X).then_inc(rank_done, 1)
                        dve.wait_ge(rank_done, i - 1)
                        dve.tensor_scalar(onehot[:], desc, rank[:, 0:1], None, ALU.is_equal).then_inc(onehot_done, 1)
                        dve.tensor_scalar(base[:], rank[:], -float(CAP), float(E * CAP), ALU.mult, ALU.add
                                          ).then_inc(base_done, 1)
                    if g == 6 and back2:
                        dve.wait_ge(px_done, i - 1)
                        dve.tensor_tensor_reduce(px_prod[:], small_ps[:, PX:PX + E], onehot[:], 1.0, 0.0,
                                                 ALU.mult, ALU.add, pos[:]).then_inc(pos_done, 1)
                        dve.tensor_tensor(carry[:], carry[:], onehot[:], ALU.add).then_inc(carry_done, 1)
                        dve.wait_ge(pos_done, i - 1)
                        dve.tensor_scalar(over[:], pos[:], float(CAP), float(SKIP), ALU.is_ge, ALU.mult
                                          ).then_inc(over_done, 1)
                        dve.wait_ge(base_done, i - 1)
                        dve.tensor_tensor(slot_f[:], pos[:], base[:], ALU.add).then_inc(slot_f_done, 1)
                    if g == 7 and back2:
                        dve.wait_ge(token_next, i - 1)
                        dve.tensor_copy(row[:, p, D + 3:D + 4].bitcast(I32), token[:]).then_inc(token_written, 1)
                        dve.wait_ge(token_written, i - 1)
                        dve.tensor_scalar(token[:], token[:], float(P), None, ALU.add).then_inc(token_next, 1)
                        dve.wait_ge(l_exped, i - 1)
                        dve.reciprocal(row[:, p, D + 2:D + 3], l_sum[:])
                        dve.wait_ge(over_done, i - 1)
                        dve.wait_ge(slot_f_done, i - 1)
                        dve.tensor_tensor(slot[:, p], slot_f[:], over[:], ALU.add).then_inc(row_ready, 1)
                if back1:
                    half = D // 2
                    dve.wait_ge(q_cast, i)
                    dve.wait_ge(k_cast, i)
                    for n in range(2):
                        dve.tensor_tensor(qk_cos[:, n], qk[:, n], cos, ALU.mult)
                        dve.tensor_tensor(qk_sin[:, n, 0:half], qk[:, n, half:D], sin[:, 0:half], ALU.mult)
                        r = dve.tensor_tensor(qk_sin[:, n, half:D], qk[:, n, 0:half], sin[:, half:D], ALU.mult)
                        if n == 0:
                            r.then_inc(rope_parts, 1)
                        else:
                            r.then_inc(rope_parts, 2)
                    dve.wait_ge(rope_parts, 3 * i)
                    after(dve, st_done, i - 1)
                    dve.tensor_tensor(qk_rot[:, :, :], qk_cos[:, :, :], qk_sin[:, :, :], ALU.add).then_inc(roped, 1)
                if cur:
                    lo(flat(att_t, 1), ua_ps[:, :], flat(att_t, 0), att_hi, i + 1, att_lo)
                if ahead:
                    lo(flat(p_t, 1), tr_ps[:, :], flat(p_t, 0), p_hi, i + 2, p_lo)
                if back1:
                    dve.wait_ge(st_done, i)
                    after(dve, exp_done, i - 1)
                    dve.scalar_tensor_tensor(out=masked[:], in0=small_ps[:, ST:ST + P], scalar=float(D) ** -0.5,
                                             in1=mask, op0=ALU.mult, op1=ALU.add).then_inc(masked_done, 1)
                if cur:
                    dve.wait_ge(out_done, i + 1)
                    dve.wait_ge(rden_scaled, i + 1)
                    dve.scalar_tensor_tensor(out=pre[:], in0=of_ps[:, :], scalar=rden[:, 0:1], in1=b_full[:],
                                             op0=ALU.mult, op1=ALU.add).then_inc(pre_done, 1)
                    dve.wait_ge(pre_done, i + 1)
                    dve.scalar_tensor_tensor(out=x1[:, p], in0=pre[:], scalar=0.0, in1=x_in[:, p],
                                             op0=ALU.max, op1=ALU.add).then_inc(x1_done, 1)
                    dve.wait_ge(x1_done, i + 1)
                    after(dve, ln_hat[1], i)
                    norm_stats(1, i, x1[:, p], stats[:, 1], mv[:, 1])
                if ahead:
                    lo(flat(u_t, 1), ua_ps[:, :], flat(u_t, 0), u_hi, i + 2, u_lo, scale=1.0 / WS)

            each_step(dve, step)

            def rows_lo(e, k, p):
                lo(flat(e_t, 1), tr_ps[:, :], flat(e_t, 0), e_hi, e + 1, e_lo)
                dve.wait_ge(e_loaded[p], 16 * (k + 1))
                dve.tensor_scalar(gate_e[p], e_row[p][:, D + 2:D + 3], 1.0 / WS, None, ALU.mult).then_inc(gate_done, 1)
                dve.wait_ge(e_idx, e + 1)
                dve.tensor_scalar(is_e, p_index, e_index[:, 0:1], None, ALU.is_equal).then_inc(e_sel_steps, 1)
                dve.wait_ge(e_sel_steps, e + 1)
                dve.tensor_scalar(sel, ones16, is_e[:, 0:1], None, ALU.mult).then_inc(e_sel, 1)
                dve.tensor_scalar(e_index, e_index, 1.0, None, ALU.add).then_inc(e_idx, 1)

            def expert(e, k, p, last):
                for kk, (which, hb) in enumerate(ORDER):
                    w = w_split[kk % SPLIT_SLOTS]
                    if kk in HI_ON_DVE:
                        dve.wait_ge(w_in[kk], 16 * (e + 1))
                        after(dve, w_used, 8 * e + kk - SPLIT_SLOTS + 1)
                        dve.tensor_scalar(w[:, 0], raw[kk], WS, None, ALU.mult).then_inc(w_hi[kk], 1)
                    if kk not in LO_ON_POOL:
                        lo(w[:, 1], raw[kk], w[:, 0], w_hi[kk], e + 1, w_lo[kk], scale=WS)
                    for hb in {2: (0,), 3: (1,), 5: (2,), 6: (3,)}.get(kk, ()):
                        n = 4 * e + hb
                        dve.wait_ge(h_relu, n + 1)
                        dve.tensor_copy(hid_split[hb][:, 0], hid[hb % 2]).then_inc(h_hi, 1)
                        lo(hid_split[hb][:, 1], hid[hb % 2], hid_split[hb][:, 0], h_hi, n + 1, h_lo)
                if not last:
                    kn, pn = neighbour(k, p, 1)
                    rows_lo(e + 1, kn, pn)
                dve.wait_ge(w_used, CHUNKS * (e + 1))
                dve.wait_ge(gate_done, e + 1)
                after(dve, out_scat[p], 16 * k)
                dve.scalar_tensor_tensor(out=o_row[p], in0=y_ps[:, :], scalar=gate_e[p][:, 0:1],
                                         in1=e_row[p][:, 0:D], op0=ALU.mult, op1=ALU.add).then_inc(y_out, 1)

            dve.wait_ge(k_done, TILES)
            dve.memset(e_index, 0.0).then_inc(e_idx, 1)
            rows_lo(0, 0, 0)
            each_expert(dve, expert)

        @block.gpsimd
        def _(pool):
            def rstd(n, t, moments):
                v, y, h = (newton[:, n, m:m + 1] for m in range(3))
                at = 11 * t
                alone(pool, ln_mv[n], t + 1)
                pool.tensor_scalar(v, moments[:, 1:2], EPS, 1.0, ALU.add, ALU.mult).then_inc(ln_step[n], 1)
                alone(pool, ln_step[n], at + 1)
                pool.tensor_scalar(y.bitcast(I32), v.bitcast(I32), -0.5, float(RSQRT_MAGIC), ALU.mult, ALU.add
                                   ).then_inc(ln_step[n], 1)
                for s in range(3):
                    alone(pool, ln_step[n], at + 3 * s + 2)
                    pool.tensor_scalar(h, y, v, y, ALU.mult, ALU.mult).then_inc(ln_step[n], 1)
                    alone(pool, ln_step[n], at + 3 * s + 3)
                    pool.tensor_scalar(h, h, -0.5, 1.5, ALU.mult, ALU.add).then_inc(ln_step[n], 1)
                    alone(pool, ln_step[n], at + 3 * s + 4)
                    pool.tensor_tensor(moments[:, 1:2] if s == 2 else y, y, h, ALU.mult).then_inc(ln_step[n], 1)
                alone(pool, ln_step[n], at + 11)

            def normalise(n, t, source, moments, dst, freed, count):
                rstd(n, t, moments)
                alone(pool, freed, count)
                pool.tensor_scalar(dst, source, moments[:, 0:1], moments[:, 1:2], ALU.subtract, ALU.mult
                                   ).then_inc(ln_hat[n], 1)

            pool.memset(fill[:, 0:D + 3], 0.0)
            pool.memset(fill[:, D + 3:D + 4].bitcast(I32), SKIP).then_inc(filled, 1)

            def step(i, k, p, ahead, cur, back1, back2):
                ka, pa = neighbour(k, p, 1)
                if back2:
                    normalise(2, i - 2, row[:, p, 0:D], row[:, p, D:D + 2], x3_hat[:], x3_tr, i - 2)
                    pool.dma_start(out[bass.ds((i - 2) * P, P), :], row[:, p, 0:D]).then_inc(base_out[p], 16)
                if ahead:
                    normalise(0, i + 1, x_in[:, pa], mv[:, 0], p_hat[:], p_tr, i + 1)
                if back2:
                    alone(pool, row_ready, i - 1)
                    if isinstance(i, int) and i == 2:
                        alone(pool, filled, 1 + 16 * (E * CAP // P))
                    alone(pool, scattered[1 - p], 16 * neighbour(k, p, -1)[0])
                    pool.indirect_dma_start(
                        out=slot_table, out_offset=bass.IndirectOffsetOnAxis(ap=slot[:, p].bitcast(U32), axis=0),
                        in_=row[:, p, :], in_offset=None, bounds_check=E * CAP - 1, oob_is_err=False,
                    ).then_inc(scattered[p], 16)
                if ahead:
                    for j in range(2):
                        alone(pool, nat_hi, 2 * (i + 1) + j + 1)
                        pool.tensor_tensor(ctx_nat[j][:, 1], ctx_raw[j], ctx_nat[j][:, 0], ALU.subtract
                                           ).then_inc(nat_lo, 1)
                        if j == 0 and cur:
                            normalise(1, i, x1[:, p], mv[:, 1], x2_hat[:], x2_tr, i)
                elif cur:
                    normalise(1, i, x1[:, p], mv[:, 1], x2_hat[:], x2_tr, i)

            each_step(pool, step)

            def rows_hat(e, k, p):
                alone(pool, e_loaded[p], 16 * (k + 1))
                alone(pool, e_tr, e)
                pool.tensor_scalar(e_hat, e_row[p][:, 0:D], e_row[p][:, D:D + 1], e_row[p][:, D + 1:D + 2],
                                   ALU.subtract, ALU.mult).then_inc(e_norm, 1)

            def scale_chunk(e, kk):
                alone(pool, w_in[kk], 16 * (e + 1))
                pool.tensor_scalar(raw[kk], raw[kk], WS, 1.0, ALU.mult, ALU.mult).then_inc(w_scaled[kk], 1)

            def expert(e, k, p, last):
                for kk, (which, hb) in enumerate(ORDER):
                    w = w_split[kk % SPLIT_SLOTS]
                    if kk in LO_ON_POOL:
                        alone(pool, w_hi[kk], e + 1)
                        pool.tensor_tensor(w[:, 1], raw[kk], w[:, 0], ALU.subtract).then_inc(w_lo[kk], 1)
                    if kk in LO_ON_POOL[:-1]:
                        scale_chunk(e, LO_ON_POOL[LO_ON_POOL.index(kk) + 1])
                    if kk == LO_ON_POOL[-1] and not last:
                        scale_chunk(e + 1, LO_ON_POOL[0])
                    if kk == 4 and not last:
                        kn, pn = neighbour(k, p, 1)
                        rows_hat(e + 1, kn, pn)
                alone(pool, y_out, e + 1)
                alone(pool, out_scat[1 - p], 16 * (neighbour(k, p, -1)[0] + 1))
                pool.indirect_dma_start(
                    out=out, out_offset=bass.IndirectOffsetOnAxis(ap=e_row[p][:, D + 3:D + 4].bitcast(U32), axis=0),
                    in_=o_row[p], in_offset=None, bounds_check=TOK - 1, oob_is_err=False,
                ).then_inc(out_scat[p], 16)

            scale_chunk(0, LO_ON_POOL[0])
            rows_hat(0, 0, 0)
            for n in range(2):
                alone(pool, base_out[n], 16 * (TILES // 2))
            each_expert(pool, expert)
            for n in range(2):
                alone(pool, out_scat[n], 16 * (E // 2))


def tables():
    k, q = np.arange(P)[:, None], np.arange(P)[None, :]
    mask = np.where((k // L == q // L) & (k <= q), 0.0, NEG).astype(np.float32)
    desc = np.broadcast_to(E - np.arange(E, dtype=np.float32), (P, E))
    f32 = np.concatenate([np.eye(P, dtype=np.float32), mask, desc, np.arange(P, dtype=np.float32)[:, None]], 1)
    inv = (np.float32(ROPE_BASE) ** (-np.arange(0, D, 2, dtype=np.float32) / np.float32(D))).astype(np.float32)
    angle = np.arange(L, dtype=np.float32)[None, :] * inv[:, None]
    parts = []
    for f, sign in ((np.cos, (1, 1)), (np.sin, (-1, 1))):
        v = f(angle).astype(np.float32).reshape(C // 2, P, L).transpose(1, 0, 2)
        v = np.concatenate([sign[0] * v, sign[1] * v], 1)
        parts.append(np.concatenate([v, v], 2).reshape(P, D))
    parts += [(k < q).astype(np.float32), np.ones((P, P), np.float32)]
    return np.ascontiguousarray(f32), np.concatenate(parts, 1)


def kernel(**inputs):
    import ml_dtypes
    from concourse import bacc
    from concourse.bass_utils import run_bass_kernel_spmd

    def a(name):
        return np.asarray(inputs[name])

    f32, f16 = tables()
    w = a("L0_xattn_W")
    arrays = {
        "x": a("x").reshape(TOK, D),
        "ctx": a("ctx_1024"),
        "w_nat": w,
        "w_t": w.T,
        "wq_t": a("L0_attn_Wq").T,
        "wk_t": a("L0_attn_Wk").T,
        "b_row": a("L0_xattn_b"),
        "b_col": a("L0_xattn_b").reshape(C, P).T,
        "fc1_w": a("L0_attn_fc1_w").reshape(INNER),
        "fc1_b": a("L0_attn_fc1_b").reshape(INNER, 1),
        "fc2_t": a("L0_attn_fc2_w").T,
        "fc2_b": a("L0_attn_fc2_b").reshape(1, D),
        "wg": a("L0_ffn_Wg"),
        "bg": a("L0_ffn_bg"),
        "w1": a("L0_ffn_W1"),
        "b1": a("L0_ffn_b1").reshape(E, H // P, P).transpose(0, 2, 1),
        "w2": a("L0_ffn_W2"),
        "b2": a("L0_ffn_b2"),
        "consts": f32,
        "consts16": f16.astype(ml_dtypes.bfloat16),
    }
    arrays = {n: np.ascontiguousarray(v) for n, v in arrays.items()}
    nc = bacc.Bacc("TRN2", target_bir_lowering=False, num_devices=1)
    args = {n: nc.dram_tensor(n, v.shape, mybir.dt.from_np(v.dtype), kind="ExternalInput").ap()
            for n, v in arrays.items()}
    out = nc.dram_tensor("out", [TOK, D], F32, kind="ExternalOutput").ap()
    program(nc, out=out, **args)
    r = run_bass_kernel_spmd(nc, [arrays], core_ids=[0])
    return r.results[0]["out"].reshape(B, L, D)
```

```python
from contextlib import ExitStack

import numpy as np

import concourse.bass as bass
from concourse import mybir

F32 = mybir.dt.float32
F16 = mybir.dt.float16
BF16 = mybir.dt.bfloat16
I32 = mybir.dt.int32
U32 = mybir.dt.uint32
ALU = mybir.AluOpType
ACT = mybir.ActivationFunctionType
AX_X = mybir.AxisListType.X

P = 128
B = 32
L = 64
D = 512
LQ = 512
C = D // P
E = 16
H = 2048
INNER = 16
TOK = B * L
TILES = TOK // P
CAP = -(-TOK // E)
HB = H // D
ROPE_BASE = 32.0
EPS = 1e-5
WS = 64.0
ROW = D + 4
SKIP = 1 << 20
RSQRT_MAGIC = 0x5F1FFFF9
RSQRT_FACTOR, RSQRT_TERM = 0.703952253, 2.38924456
RSQRT_STEPS = 9
NEG = -1e30

ORDER = [(1, 0), (1, 1), (2, 0), (1, 2), (1, 3), (2, 1), (2, 2), (2, 3)]
CHUNKS = len(ORDER)
SPLIT_SLOTS = 4
LO_ON_POOL = (1, 4, 6)

PB, H1 = 0, 128
RT, PX = 0, 16


def program(nc, x, ctx, ctx_tr, w_nat, w_t, wq_t, wk_t, b_row, b_col, fc1_w, fc1_b, fc2_t, fc2_b, wg, bg,
            w1, b1, w2, b2, consts, consts16, out):
    with ExitStack() as stack:
        def sb(name, shape, dt):
            return stack.enter_context(nc.sbuf_tensor(name, shape, dt))

        def sem(name):
            return stack.enter_context(nc.semaphore(name))

        def bank(name):
            return stack.enter_context(nc.psum_tensor(name, [P, 512], F32))

        def after(eng, semaphore, count):
            if not isinstance(count, int) or count > 0:
                eng.wait_ge(semaphore, count)

        def alone(eng, semaphore, count):
            after(eng, semaphore, count)
            if not isinstance(count, int):
                eng.sem_inc(passed, 1)

        slot_table = nc.dram_tensor("slot_table", [E * CAP, ROW], F32, kind="Internal").ap()

        raw_low = sb("raw_weights_0_3", [P, 4, 4, D], F32)
        arena = sb("raw_context_then_raw_weights_4_7", [P, 4, 4, D], F32)
        split_arena = sb("raw_projections_then_split_weights", [P, 4, 4, D], F32)
        proj_arena = sb("projections_then_expert_tiles", [P, 4, 4 * D], F32)
        ctx_t = sb("context_transposed", [P, 2, 2, C, LQ], F16)
        ctx_nat = sb("context_natural", [P, 2, 2, C, D], F16)

        raw = [raw_low[:, n] for n in range(4)] + [arena[:, n] for n in range(4)]
        ctx_t_raw = [arena[:, j] for j in range(2)]
        ctx_raw = [arena[:, 2 + j] for j in range(2)]
        proj_raw = [split_arena[:, n] for n in range(4)]
        w_split = [split_arena[:, n].rearrange("p c d -> p (c d)").bitcast(F16)
                   .rearrange("p (s c d) -> p s c d", s=2, c=4) for n in range(SPLIT_SLOTS)]
        proj = [proj_arena[:, n].bitcast(F16).rearrange("p (s c d) -> p s c d", s=2, c=4) for n in range(4)]
        W_U, W_O, W_Q, W_K = proj

        x_in = sb("x_in", [P, 2, D], F32)
        hat13 = sb("first_and_third_norm", [P, D], F32)
        p_t = sb("p_transposed", [P, 2, C, P], F16)
        u_t = sb("u_transposed", [P, 2, C, P], F16)
        probs = sb("second_norm_then_probs", [P, LQ], F32)
        x2_hat = probs
        probs_t = sb("probs_transposed", [P, 2, C, P], F16)
        att_t = sb("att_transposed", [P, 2, C, P], F16)
        x1 = sb("x1", [P, 2, D], F32)
        x2_t = sb("x2_transposed", [P, 2, C, P], F16)
        qk = sb("qk", [P, 2, D], BF16)
        qk_rot = sb("qk_rotated", [P, 2, D], BF16)
        masked = sb("masked_scores", [P, P], F32)
        exp_t = sb("exp_scores", [P, P], F32)
        inner = sb("inner", [P, P], F32)
        row = sb("rows_for_slots", [P, 2, ROW], F32)
        fill = row[:, 1]
        x3_t = sb("x3_transposed", [P, 2, C, P], F16)

        cst = sb("tables_f32", [P, 2 * P + E + 1], F32)
        ident, mask = cst[:, 0:P], cst[:, P:2 * P]
        desc, p_index = cst[:, 2 * P:2 * P + E], cst[:, 2 * P + E:2 * P + E + 1]
        cst16 = sb("tables_bf16", [P, 2 * D + 2 * P], BF16)
        cos, sin = cst16[:, 0:D], cst16[:, D:2 * D]
        before, ones16 = cst16[:, 2 * D:2 * D + P], cst16[:, 2 * D + P:2 * D + 2 * P]
        b_full = sb("b_on_all_partitions", [P, D], F32)
        b_raw = sb("b_column", [P, C], F32)
        b_split = sb("b_column_split", [P, 2, C], F16)
        fc1_rows = sb("fc1_on_all_rows", [P, P], F32)
        fc1_bias = sb("fc1_bias", [P, 1], F32)
        fc2 = sb("fc2", [P, D], F32)
        wg_raw = sb("wg_raw", [P, C, E], F32)
        wg_split = sb("wg_split", [P, 2, C, E], F16)
        bg_full = sb("bg_on_all_partitions", [P, E], F32)

        stats = sb("stats", [P, 3, 6], F32)
        mv = sb("mean_var", [P, 2, 2], F32)
        newton = sb("newton", [P, 3, 3], F32)
        small = sb("small", [P, 12], F32)
        (s_max, s_max_b, s_shift, den, rden, l_max, l_neg, l_sum, rank, pos, base, over) = (
            small[:, n:n + 1] for n in range(12))
        slot_f = sb("slot_before_capacity", [P, 1], F32)
        logits = sb("logits", [P, E], F32)
        l_exp = sb("logit_exp", [P, E], F32)
        cand = sb("candidates", [P, E], F32)
        onehot = sb("onehot", [P, E], BF16)
        carry = sb("tokens_so_far", [P, E], BF16)
        px_prod = sb("position_product", [P, E], F32)
        slot = sb("slot", [P, 2, 1], I32)
        token = sb("token", [P, 1], F32)

        ffn = proj_arena[:, :].rearrange("p a b -> p (a b)")
        taken = [0]

        def carve(n):
            at = taken[0]
            taken[0] = at + n
            assert taken[0] <= 16 * D
            return ffn[:, at:at + n]

        e_row = [carve(ROW) for _ in range(2)]
        e_hat = carve(D)
        e_t = carve(D).bitcast(F16).rearrange("p (s c n) -> p s c n", s=2, c=C)
        hid = [carve(D) for _ in range(2)]
        hid_split = [carve(D).bitcast(F16).rearrange("p (s n) -> p s n", s=2) for _ in range(HB)]
        o_row = [carve(D) for _ in range(2)]
        b2_raw = carve(D)
        b2_split = carve(D).bitcast(F16).rearrange("p (s n) -> p s n", s=2)
        b1_e = [carve(H // P) for _ in range(2)]
        gate_e = [carve(1) for _ in range(2)]
        sel = carve(P // 2).bitcast(F16)
        is_e = carve(1)
        e_index = carve(1)

        scores_ps = bank("scores_ps")
        tr_a = bank("transposes_a_ps")
        tr_b = bank("transposes_b_ps")
        ua_ps = bank("u_att_ps")
        q_ps = bank("q_routing_ps")
        k_ps = bank("k_self_scores_ps")
        of_ps = bank("out_fc2_ps")
        small_ps = bank("small_ps")
        hid_ps = [q_ps, k_ps]
        y_ps = of_ps

        passed = sem("waits_passed")
        consts_in = sem("consts_in")
        smalls_in = sem("small_inputs_in")
        begun = sem("begun")
        proj_in = [sem(f"proj_in{n}") for n in range(4)]
        proj_hi = sem("proj_hi")
        proj_lo = sem("proj_lo")
        small_hi = sem("small_hi")
        small_lo = sem("small_lo")
        zeroed = sem("zeroed")
        padded = sem("padded")
        filled = sem("table_filled")
        x_loaded = [sem(f"x_loaded{n}") for n in range(2)]
        ctx_loaded = [sem(f"ctx_loaded{n}") for n in range(2)]
        ctx_t_loaded = [sem(f"ctx_t_loaded{n}") for n in range(2)]
        ln_stats = [sem(f"ln{n}_stats") for n in range(3)]
        ln_mv = [sem(f"ln{n}_mean_var") for n in range(3)]
        ln_step = [sem(f"ln{n}_rsqrt_steps") for n in range(3)]
        ln_hat = [sem(f"ln{n}_normalised") for n in range(3)]
        p_tr = sem("p_transposes")
        p_hi = sem("p_hi")
        p_lo = sem("p_lo")
        u_done = sem("u_done")
        u_hi = sem("u_hi")
        u_lo = sem("u_lo")
        pb_done = sem("pb_done")
        ctx_hi = sem("ctx_t_hi_halves")
        ctx_lo = sem("ctx_t_lo_quarters")
        nat_hi = sem("ctx_natural_hi_batches")
        nat_lo = sem("ctx_natural_lo_batches")
        s_done = sem("scores_done")
        s_maxed = sem("scores_maxed")
        s_biased = sem("scores_max_biased")
        s_shifted = sem("scores_shift")
        p_exp = sem("probs_exp")
        rden_ready = sem("rden_ready")
        rden_scaled = sem("rden_scaled")
        pt_tr = sem("probs_transposes")
        pt_hi = sem("probs_hi")
        pt_lo = sem("probs_lo")
        att_done = sem("att_done")
        att_hi = sem("att_hi")
        att_lo = sem("att_lo")
        out_done = sem("out_done")
        pre_done = sem("pre_relu_done")
        b2_in, b2_zero, b2_hi, b2_lo = (sem(n) for n in ("b2_in", "b2_zeroed", "b2_hi", "b2_lo"))
        x1_done = sem("x1_done")
        x2_tr = sem("x2_transposes")
        x2_hi = sem("x2_hi")
        x2_lo = sem("x2_lo")
        q_done = sem("q_done")
        k_done = sem("k_done")
        q_cast = sem("q_cast")
        k_cast = sem("k_cast")
        rope_sin = sem("rope_sin")
        rope_cos = sem("rope_cos")
        roped = sem("roped")
        st_done = sem("st_done")
        masked_done = sem("masked_done")
        exp_done = sem("exp_done")
        h1_done = sem("h1_done")
        inner_done = sem("inner_done")
        fc2_done = sem("fc2_done")
        x2_done = sem("x2_done")
        x3_tr = sem("x3_transposes")
        x3_hi = sem("x3_hi")
        x3_lo = sem("x3_lo")
        logits_mm = sem("logits_mm")
        logits_done = sem("logits_done")
        l_maxed = sem("logits_maxed")
        l_negated = sem("logits_max_negated")
        l_exped = sem("logits_exp")
        cand_done = sem("candidates_done")
        rank_done = sem("rank_done")
        onehot_done = sem("onehot_done")
        px_done = sem("prefix_done")
        carry_done = sem("carry_done")
        pos_done = sem("position_done")
        base_done = sem("first_slot_done")
        over_done = sem("over_done")
        slot_f_done = sem("slot_f_done")
        row_ready = sem("row_ready")
        token_written = sem("token_written")
        token_next = sem("token_next")
        base_out = [sem(f"x2_stored{n}") for n in range(2)]
        scattered = [sem(f"row_scattered{n}") for n in range(2)]

        w_in = [sem(f"w_chunk_loaded{n}") for n in range(CHUNKS)]
        w_scaled = [sem(f"w_chunk_scaled{n}") for n in range(CHUNKS)]
        w_hi = [sem(f"w_chunk_hi{n}") for n in range(CHUNKS)]
        w_lo = [sem(f"w_chunk_lo{n}") for n in range(CHUNKS)]
        w_used = sem("w_chunks_used")
        e_loaded = [sem(f"expert_rows_loaded{n}") for n in range(2)]
        b1_loaded = [sem(f"b1_loaded{n}") for n in range(2)]
        e_norm = sem("expert_rows_normalised")
        e_tr = sem("expert_transposes")
        e_hi = sem("expert_rows_hi")
        e_lo = sem("expert_rows_lo")
        e_idx = sem("expert_index")
        e_sel = sem("expert_selected")
        e_sel_steps = sem("expert_select_steps")
        gate_done = sem("gate_done")
        h_relu = sem("hidden_blocks_relu")
        h_hi = sem("hidden_blocks_hi")
        h_lo = sem("hidden_blocks_lo")
        y_out = sem("y_out")
        out_scat = [sem(f"out_scattered{n}") for n in range(2)]

        block = stack.enter_context(nc.Block())

        def each_step(eng, step):
            for i in range(-1, 4):
                step(i, i // 2, i % 2, ahead=True, cur=i >= 0, back1=i >= 1, back2=i >= 2)
            with eng.Fori(2, TILES // 2 - 1) as k:
                for p in range(2):
                    step(2 * k + p, k, p, ahead=True, cur=True, back1=True, back2=True)
            for i in range(TILES - 2, TILES + 2):
                step(i, i // 2, i % 2, ahead=i < TILES - 1, cur=i < TILES, back1=i <= TILES, back2=True)

        def each_expert(eng, expert):
            for p in range(2):
                expert(p, 0, p, False)
            with eng.Fori(1, E // 2 - 1) as k:
                for p in range(2):
                    expert(2 * k + p, k, p, False)
            for p in range(2):
                expert(E - 2 + p, E // 2 - 1, p, p == 1)

        def neighbour(k, p, d):
            return k + (p + d) // 2, (p + d) % 2

        def chunk_source(e, kk):
            which, hb = ORDER[kk]
            return (w1 if which == 1 else w2)[bass.ds(e, 1), hb].rearrange("o p c d -> (o p) c d")

        def later(e, kk):
            return (e, kk + SPLIT_SLOTS) if kk + SPLIT_SLOTS < CHUNKS else (e + 1, kk + SPLIT_SLOTS - CHUNKS)

        def rstd(eng, n, t, moments):
            v, y, h = (newton[:, n, m:m + 1] for m in range(3))
            at = RSQRT_STEPS * t
            done = ln_step[n]
            eng.tensor_scalar(v, moments[:, 1:2], EPS, 1.0, ALU.add, ALU.mult).then_inc(done, 1)
            alone(eng, done, at + 1)
            eng.tensor_scalar(y.bitcast(I32), v.bitcast(I32), -0.5, float(RSQRT_MAGIC), ALU.mult, ALU.add
                              ).then_inc(done, 1)
            alone(eng, done, at + 2)
            eng.tensor_scalar(h, y, v, y, ALU.mult, ALU.mult).then_inc(done, 1)
            alone(eng, done, at + 3)
            eng.tensor_scalar(h, h, -RSQRT_FACTOR, RSQRT_FACTOR * RSQRT_TERM, ALU.mult, ALU.add).then_inc(done, 1)
            alone(eng, done, at + 4)
            eng.tensor_tensor(y, y, h, ALU.mult).then_inc(done, 1)
            alone(eng, done, at + 5)
            eng.tensor_scalar(h, y, v, y, ALU.mult, ALU.mult).then_inc(done, 1)
            alone(eng, done, at + 6)
            eng.tensor_scalar(v, h, 0.375, -1.25, ALU.mult, ALU.add).then_inc(done, 1)
            alone(eng, done, at + 7)
            eng.tensor_scalar(v, v, h, 1.875, ALU.mult, ALU.add).then_inc(done, 1)
            alone(eng, done, at + 8)
            eng.tensor_tensor(moments[:, 1:2], y, v, ALU.mult).then_inc(done, 1)

        @block.sync
        def _(sp):
            def load_tile(t, k, p, what):
                if what == "x":
                    after(sp, x1_done, t - 1)
                    sp.dma_start(x_in[:, p], x[bass.ds(t * P, P), :]).then_inc(x_loaded[p], 16)
                for j in range(2):
                    if what == "t":
                        alone(sp, ctx_lo, 8 * (t - 1) + 4 * j + 4)
                        sp.dma_start(ctx_t_raw[j], ctx_tr[bass.ds(2 * t + j, 1)].rearrange("o p c d -> (o p) c d")
                                     ).then_inc(ctx_t_loaded[j], 16)
                    if what == "n":
                        alone(sp, nat_lo, 2 * (t - 1) + j + 1)
                        sp.dma_start(ctx_raw[j], ctx[bass.ds(2 * t + j, 1)].rearrange("o (p c) d -> (o p) c d", c=4)
                                     ).then_inc(ctx_loaded[j], 16)

            sp.dma_start(cst[:], consts).then_inc(consts_in, 16)
            sp.dma_start(x_in[:, 0], x[0:P, :]).then_inc(x_loaded[0], 16)

            def load_proj(n):
                w = (w_nat, w_t, wq_t, wk_t)[n]
                sp.dma_start(proj_raw[n], w.rearrange("(c p) d -> p c d", p=P)).then_inc(proj_in[n], 16)

            load_proj(0)
            for j in range(2):
                sp.dma_start(ctx_t_raw[j], ctx_tr[j]).then_inc(ctx_t_loaded[j], 16)
            sp.dma_start(b_raw[:], b_col).then_inc(smalls_in, 16)
            sp.dma_start(wg_raw[:], wg.rearrange("(c p) e -> p c e", p=P)).then_inc(smalls_in, 16)
            for j in range(2):
                sp.dma_start(ctx_raw[j], ctx[j].rearrange("(p c) d -> p c d", c=4)).then_inc(ctx_loaded[j], 16)
            load_proj(1)
            sp.dma_start(b_full[:], b_row.partition_broadcast(P)).then_inc(smalls_in, 16)
            sp.dma_start(bg_full[:], bg.partition_broadcast(P)).then_inc(smalls_in, 16)
            sp.dma_start(cst16[:], consts16).then_inc(smalls_in, 16)
            sp.dma_start(x_in[:, 1], x[P:2 * P, :]).then_inc(x_loaded[1], 16)
            sp.wait_ge(zeroed, 3)
            sp.dma_start(fc1_rows[:, 0:INNER], fc1_w.partition_broadcast(P)).then_inc(padded, 16)
            sp.dma_start(fc1_bias[0:INNER, :], fc1_b).then_inc(padded, 16)
            sp.dma_start(fc2[0:INNER, :], fc2_t).then_inc(padded, 16)
            sp.dma_start(fc2[32:33, :], fc2_b).then_inc(padded, 16)

            def step(i, k, p, ahead, cur, back1, back2):
                if isinstance(i, int) and i == -1:
                    load_tile(1, 0, 1, "t")
                    load_proj(2)
                    load_proj(3)
                    load_tile(1, 0, 1, "n")
                elif not isinstance(i, int) or i + 2 < TILES:
                    for what in "xtn":
                        load_tile(i + 2, k + 1, p, what)
                if isinstance(i, int) and i == -1:
                    sp.wait_ge(begun, 2)
                    for n in range(E * CAP // P):
                        sp.dma_start(slot_table[n * P:(n + 1) * P, :], fill).then_inc(filled, 16)
                if isinstance(i, int) and i == 1:
                    for kk in range(4):
                        sp.dma_start(raw[kk], chunk_source(0, kk)).then_inc(w_in[kk], 16)
                if isinstance(i, int) and i == TILES - 2:
                    for kk in range(4):
                        sp.wait_ge(w_lo[kk], 1)
                        sp.dma_start(raw[kk], chunk_source(1, kk)).then_inc(w_in[kk], 16)

            each_step(sp, step)

            def load_rows(e, k, p):
                alone(sp, out_scat[p], 16 * k)
                sp.dma_start(e_row[p], slot_table[bass.ds(e * CAP, CAP), :]).then_inc(e_loaded[p], 16)
                sp.dma_start(b1_e[p], b1[bass.ds(e, 1)].rearrange("o p c -> (o p) c")).then_inc(b1_loaded[p], 16)

            def load_chunk(e, kk):
                alone(sp, w_lo[kk], e)
                sp.dma_start(raw[kk], chunk_source(e, kk)).then_inc(w_in[kk], 16)

            for kk in range(4, CHUNKS):
                if kk < 6:
                    sp.wait_ge(ctx_lo, 8 * (TILES - 1) + 4 * (kk - 4) + 4)
                else:
                    sp.wait_ge(nat_lo, 2 * (TILES - 1) + kk - 6 + 1)
                sp.dma_start(raw[kk], chunk_source(0, kk)).then_inc(w_in[kk], 16)
            sp.wait_ge(b2_zero, 1)
            sp.dma_start(b2_raw[0:E, :], b2).then_inc(b2_in, 16)
            for n in range(2):
                sp.wait_ge(scattered[n], 16 * (TILES // 2))
            load_rows(0, 0, 0)
            load_rows(1, 0, 1)
            for kk in range(4, CHUNKS):
                load_chunk(1, kk)
            with sp.Fori(1, E // 2) as k:
                for p in range(2):
                    for kk in range(CHUNKS):
                        load_chunk(2 * k + p, kk)
                        if kk == 3:
                            load_rows(2 * k + p, k, p)

        @block.tensor
        def _(pe):
            def three(out_ps, left, right, first, last):
                pe.matmul(out_ps, left[0], right[0], start=first, stop=False)
                pe.matmul(out_ps, left[0], right[1], start=False, stop=False)
                return pe.matmul(out_ps, left[1], right[0], start=False, stop=last)

            def both(a, *at):
                return (a[(slice(None), 0) + at], a[(slice(None), 1) + at])

            def transpose4(dst, source):
                for c in range(C):
                    mm = pe.transpose(dst[:, c * P:(c + 1) * P], source[:, c * P:(c + 1) * P], ident)
                return mm

            def cols(c):
                return slice(c * P, (c + 1) * P)

            A = slice(None)

            def score_chunks(chunks):
                for c in chunks:
                    for n, (a, b) in enumerate(((0, 0), (0, 1), (1, 0))):
                        for j in range(2):
                            mm = pe.matmul(scores_ps[j * L:(j + 1) * L, :], u_t[:, a, c, j * L:(j + 1) * L],
                                           ctx_t[:, j, b, c, :], start=(c == 0 and n == 0),
                                           stop=(c == C - 1 and n == 2))
                return mm

            def project(ps, w):
                for oc in range(C):
                    for c in range(C):
                        mm = three(ps[:, cols(oc)], both(w, c, cols(oc)), both(x2_t, c, A), c == 0, c == C - 1)
                return mm

            def step(i, k, p, ahead, cur, back1, back2):
                if cur:
                    pe.wait_ge(u_lo, i + 1)
                    pe.wait_ge(ctx_lo, 8 * (i + 1))
                    after(pe, p_exp, i)
                    score_chunks((0, 1))
                if back1:
                    pe.wait_ge(ln_hat[1], i)
                    pe.wait_ge(pt_lo, i)
                    transpose4(tr_a, x2_hat).then_inc(x2_tr, 1)
                if cur:
                    score_chunks((2, 3)).then_inc(s_done, 1)
                if back1:
                    pe.wait_ge(x2_lo, i)
                    if back2:
                        pe.wait_ge(pos_done, i - 2) if not isinstance(i, int) or i > 2 else None
                    if isinstance(i, int) and i == 1:
                        pe.wait_ge(proj_lo, 3)
                    project(q_ps, W_Q).then_inc(q_done, 1)
                if cur:
                    pe.wait_ge(p_exp, i + 1)
                    if back1:
                        pe.wait_ge(x2_lo, i)
                    transpose4(tr_a, probs).then_inc(pt_tr, 1)
                if back1:
                    after(pe, masked_done, i - 1)
                    if isinstance(i, int) and i == 1:
                        pe.wait_ge(proj_lo, 4)
                    project(k_ps, W_K).then_inc(k_done, 1)
                if back2:
                    pe.wait_ge(ln_hat[2], i - 1)
                    pe.wait_ge(p_lo, min(i + 1, TILES) if isinstance(i, int) else i + 1)
                    transpose4(tr_b, hat13[:]).then_inc(x3_tr, 1)
                if cur:
                    pe.wait_ge(pt_lo, i + 1)
                    pe.wait_ge(nat_lo, 2 * i + 2)
                    pe.wait_ge(u_lo, i + 1)
                    for j in range(2):
                        for hc in range(C):
                            for c in range(C):
                                mm = three(ua_ps[:, hc * P + j * L:hc * P + (j + 1) * L],
                                           both(ctx_nat[:, j], c, cols(hc)), both(probs_t, c, slice(j * L, (j + 1) * L)),
                                           c == 0, c == C - 1)
                    mm.then_inc(att_done, 1)
                if back2:
                    pe.wait_ge(x3_lo, i - 1)
                    pe.wait_ge(q_cast, min(i, TILES) if isinstance(i, int) else i)
                    for c in range(C):
                        mm = three(q_ps[:, RT:RT + E], both(x3_t, c, A), both(wg_split, c, A), c == 0, c == C - 1)
                    mm.then_inc(logits_mm, 1)
                if ahead:
                    pe.wait_ge(ln_hat[0], i + 2)
                    if back2:
                        pe.wait_ge(x3_lo, i - 1)
                    else:
                        after(pe, p_lo, i + 1)
                    transpose4(tr_b, hat13[:]).then_inc(p_tr, 1)
                if back1:
                    pe.wait_ge(roped, i)
                    for c in range(C):
                        mm = pe.matmul(k_ps[:, 0:P], qk_rot[:, 1, cols(c)], qk_rot[:, 0, cols(c)],
                                       start=(c == 0), stop=(c == C - 1))
                    mm.then_inc(st_done, 1)
                if cur:
                    pe.wait_ge(att_lo, i + 1)
                    after(pe, x2_done, i - 1)
                    if isinstance(i, int) and i == 0:
                        pe.wait_ge(proj_lo, 2)
                    for c in range(C):
                        mm = three(of_ps[:, :], both(att_t, c, A), both(W_O, c, A), c == 0, c == C - 1)
                    mm.then_inc(out_done, 1)
                if back2:
                    pe.wait_ge(onehot_done, i - 1)
                    pe.wait_ge(carry_done, i - 1)
                    pe.matmul(q_ps[:, PX:PX + E], before, onehot[:], start=True, stop=False)
                    pe.matmul(q_ps[:, PX:PX + E], ones16, carry[:], start=False, stop=True).then_inc(px_done, 1)
                if back1:
                    pe.wait_ge(exp_done, i)
                    if cur:
                        pe.wait_ge(s_shifted, i + 1)
                    if isinstance(i, int) and i == 1:
                        pe.wait_ge(padded, 16 * 4)
                    pe.matmul(small_ps[:, H1:H1 + P], fc1_rows[:], exp_t[:], start=True, stop=True).then_inc(h1_done, 1)
                if ahead:
                    pe.wait_ge(p_lo, i + 2)
                    after(pe, att_lo, i + 1)
                    if isinstance(i, int) and i == -1:
                        pe.wait_ge(proj_lo, 1)
                        pe.wait_ge(small_lo, 1)
                    for hc in range(C):
                        for c in range(C):
                            mm = three(ua_ps[:, cols(hc)], both(W_U, c, cols(hc)), both(p_t, c, A), c == 0, c == C - 1)
                    mm.then_inc(u_done, 1)
                    if back1:
                        pe.wait_ge(inner_done, i)
                    else:
                        after(pe, s_shifted, i + 1)
                    for c in range(C):
                        mm = three(small_ps[:, PB:PB + 1], both(p_t, c, A), both(b_split, slice(c, c + 1)),
                                   c == 0, c == C - 1)
                    mm.then_inc(pb_done, 1)
                if back1:
                    pe.wait_ge(inner_done, i)
                    if cur:
                        pe.wait_ge(pre_done, i + 1)
                    else:
                        pe.wait_ge(x2_done, i - 1)
                    pe.matmul(of_ps[:, :], inner[:], fc2[:], start=True, stop=True).then_inc(fc2_done, 1)

            pe.wait_ge(consts_in, 16)
            each_step(pe, step)

            def transpose_rows(e):
                pe.wait_ge(e_norm, e + 1)
                transpose4(tr_a, e_hat).then_inc(e_tr, 1)

            def expert(e, k, p, last):
                for kk, (which, hb) in enumerate(ORDER):
                    w = w_split[kk % SPLIT_SLOTS]
                    pe.wait_ge(w_lo[kk], e + 1)
                    if which == 1:
                        if kk == 0:
                            pe.wait_ge(e_lo, e + 1)
                        n = 4 * e + hb
                        after(pe, h_relu, n - 1)
                        for hc in range(C):
                            for c in range(C):
                                mm = three(hid_ps[hb % 2][:, cols(hc)], both(w, c, cols(hc)), both(e_t, c, A),
                                           c == 0, c == C - 1)
                        mm.then_inc(w_used, 1)
                    else:
                        pe.wait_ge(h_lo, 4 * e + hb + 1)
                        if hb == 0:
                            after(pe, y_out, e)
                            pe.wait_ge(e_sel, e + 1)
                            pe.matmul(y_ps[:, :], sel, b2_split[:, 0], start=True, stop=False)
                            pe.matmul(y_ps[:, :], sel, b2_split[:, 1], start=False, stop=False)
                        for c in range(C):
                            mm = three(y_ps[:, :], both(hid_split[hb], cols(c)), both(w, c, A),
                                       False, hb == HB - 1 and c == C - 1)
                        mm.then_inc(w_used, 1)
                    if kk == 5 and not last:
                        transpose_rows(e + 1)

            transpose_rows(0)
            each_expert(pe, expert)

        @block.scalar
        def _(act):
            def hi(dst, src, produced, count, done, scale=1.0):
                act.wait_ge(produced, count)
                act.activation(dst, src, ACT.Copy, scale=scale).then_inc(done, 1)

            def flat(a, s):
                return a[:, s].rearrange("p c n -> p (c n)")

            def proj_high(n):
                hi(proj[n][:, 0], proj_raw[n], proj_in[n], 16, proj_hi, scale=WS)

            proj_high(0)
            act.wait_ge(smalls_in, 16 * 5)
            act.activation(b_split[:, 0], b_raw[:], ACT.Copy, scale=WS).then_inc(small_hi, 1)
            act.activation(wg_split[:, 0], wg_raw[:], ACT.Copy, scale=WS).then_inc(small_hi, 1)

            def context_high(t, half):
                j, c = half // 2, 2 * (half % 2)
                if half % 2 == 0:
                    act.wait_ge(ctx_t_loaded[j], 16 * (t + 1))
                act.activation(ctx_t[:, j, 0, c:c + 2], ctx_t_raw[j][:, c:c + 2], ACT.Copy).then_inc(ctx_hi, 1)

            def natural_high(t, j):
                act.wait_ge(ctx_loaded[j], 16 * (t + 1))
                act.activation(ctx_nat[:, j, 0], ctx_raw[j], ACT.Copy).then_inc(nat_hi, 1)

            def self_exp(i):
                act.wait_ge(masked_done, i)
                after(act, h1_done, i - 1)
                act.activation(exp_t[:], masked[:], ACT.Exp).then_inc(exp_done, 1)

            def step(i, k, p, ahead, cur, back1, back2):
                if back1:
                    hi(flat(x2_t, 0), tr_a[:, :], x2_tr, i, x2_hi)
                if cur:
                    act.wait_ge(s_shifted, i + 1)
                    after(act, x2_tr, i)
                    act.activation(probs[:], scores_ps[:, :], ACT.Exp, bias=s_shift, scale=1.0,
                                   accum_out=den).then_inc(p_exp, 1)
                if ahead:
                    after(act, s_done, i + 1)
                    context_high(i + 1, 0)
                if cur:
                    hi(flat(probs_t, 0), tr_a[:, :], pt_tr, i + 1, pt_hi)
                if ahead:
                    context_high(i + 1, 1)
                if back1:
                    after(act, roped, i - 1)
                    hi(qk[:, 0, :], q_ps[:, :], q_done, i, q_cast, scale=1.0 / WS)
                if ahead:
                    context_high(i + 1, 2)
                if back1:
                    hi(qk[:, 1, :], k_ps[:, :], k_done, i, k_cast, scale=1.0 / WS)
                if back2:
                    hi(flat(x3_t, 0), tr_b[:, :], x3_tr, i - 1, x3_hi)
                if ahead:
                    context_high(i + 1, 3)
                if cur:
                    hi(flat(att_t, 0), ua_ps[:, :], att_done, i + 1, att_hi)
                if ahead:
                    hi(flat(p_t, 0), tr_b[:, :], p_tr, i + 2, p_hi)
                    natural_high(i + 1, 0)
                if back1:
                    self_exp(i)
                if back2:
                    act.wait_ge(l_negated, i - 1)
                    after(act, row_ready, i - 2)
                    act.activation(l_exp[:], logits[:], ACT.Exp, bias=l_neg, scale=1.0,
                                   accum_out=l_sum).then_inc(l_exped, 1)
                if ahead:
                    natural_high(i + 1, 1)
                if back1:
                    act.wait_ge(h1_done, i)
                    after(act, fc2_done, i - 1)
                    if isinstance(i, int) and i == 1:
                        act.wait_ge(zeroed, 4)
                    act.activation(inner[:], small_ps[:, H1:H1 + P], ACT.Relu, bias=fc1_bias[:]).then_inc(inner_done, 1)
                if ahead:
                    hi(flat(u_t, 0), ua_ps[:, :], u_done, i + 2, u_hi, scale=1.0 / WS)
                if isinstance(i, int) and i == -1:
                    proj_high(1)
                    proj_high(2)
                    proj_high(3)
                if isinstance(i, int) and i == 3:
                    for kk in range(SPLIT_SLOTS):
                        chunk_high(0, kk)

            def chunk_high(e, kk):
                if kk in LO_ON_POOL:
                    act.wait_ge(w_scaled[kk], e + 1)
                else:
                    act.wait_ge(w_in[kk], 16 * (e + 1))
                after(act, w_used, CHUNKS * e + kk - SPLIT_SLOTS + 1)
                act.activation(w_split[kk % SPLIT_SLOTS][:, 0], raw[kk], ACT.Copy,
                               scale=1.0 if kk in LO_ON_POOL else WS).then_inc(w_hi[kk], 1)

            each_step(act, step)

            def rows_hi(e):
                hi(flat(e_t, 0), tr_a[:, :], e_tr, e + 1, e_hi)

            def expert(e, k, p, last):
                for kk, (which, hb) in enumerate(ORDER):
                    if which == 1:
                        act.wait_ge(w_used, CHUNKS * e + kk + 1)
                        after(act, h_lo, 4 * e + hb - 1)
                        if hb == 0:
                            act.wait_ge(b1_loaded[p], 16 * (k + 1))
                        for hc in range(C):
                            r = act.activation(hid[hb % 2][:, hc * P:(hc + 1) * P],
                                               hid_ps[hb % 2][:, hc * P:(hc + 1) * P], ACT.Relu,
                                               bias=b1_e[p][:, 4 * hb + hc:4 * hb + hc + 1], scale=1.0 / WS)
                        r.then_inc(h_relu, 1)
                    if kk < SPLIT_SLOTS or not last:
                        chunk_high(*later(e, kk))
                    if kk == 6 and not last:
                        rows_hi(e + 1)

            rows_hi(0)
            act.wait_ge(b2_in, 16)
            act.activation(b2_split[:, 0], b2_raw, ACT.Copy, scale=WS).then_inc(b2_hi, 1)
            each_expert(act, expert)

        @block.vector
        def _(dve):
            def lo(dst, src, high, done_hi, count, done, scale=1.0):
                dve.wait_ge(done_hi, count)
                if scale == 1.0:
                    dve.tensor_tensor(dst, src, high, ALU.subtract).then_inc(done, 1)
                else:
                    dve.scalar_tensor_tensor(out=dst, in0=src, scalar=scale, in1=high, op0=ALU.mult,
                                             op1=ALU.subtract).then_inc(done, 1)

            def flat(a, s):
                return a[:, s].rearrange("p c n -> p (c n)")

            def norm_stats(n, t, source, moments):
                dve.bn_stats(stats[:, n], source).then_inc(ln_stats[n], 1)
                alone(dve, ln_stats[n], t + 1)
                dve.bn_aggr(moments, stats[:, n]).then_inc(ln_mv[n], 1)

            def normalise(n, t, source, moments, dst):
                dve.wait_ge(ln_step[n], RSQRT_STEPS * (t + 1))
                dve.tensor_scalar(dst, source, moments[:, 0:1], moments[:, 1:2], ALU.subtract, ALU.mult
                                  ).then_inc(ln_hat[n], 1)

            dve.memset(fc1_rows[:], 0.0).then_inc(zeroed, 1)
            dve.memset(fc1_bias[:], 0.0).then_inc(zeroed, 1)
            dve.memset(fc2[:], 0.0).then_inc(zeroed, 1)
            dve.memset(carry[:], 0.0).then_inc(carry_done, 1)
            dve.wait_ge(zeroed, 2)
            dve.memset(fc1_bias[32:33, :], 1.0).then_inc(zeroed, 1)
            dve.wait_ge(consts_in, 16)
            dve.tensor_copy(token[:], p_index).then_inc(token_next, 1)
            dve.wait_ge(x_loaded[0], 16)
            norm_stats(0, 0, x_in[:, 0], mv[:, 0])

            def proj_low(n):
                dve.wait_ge(proj_hi, n + 1)
                dve.scalar_tensor_tensor(out=proj[n][:, 1], in0=proj_raw[n], scalar=WS, in1=proj[n][:, 0],
                                         op0=ALU.mult, op1=ALU.subtract).then_inc(proj_lo, 1)

            def step(i, k, p, ahead, cur, back1, back2):
                ka, pa = neighbour(k, p, 1)
                half = D // 2
                starting = isinstance(i, int) and i == -1

                def context_low(n):
                    if ahead:
                        j, c = n // 4, n % 4
                        lo(ctx_t[:, j, 1, c], ctx_t_raw[j][:, c], ctx_t[:, j, 0, c],
                           ctx_hi, 4 * (i + 1) + n // 2 + 1, ctx_lo)

                if back2:
                    dve.wait_ge(fc2_done, i - 1)
                    after(dve, scattered[p], 16 * (k - 1))
                    after(dve, base_out[p], 16 * (k - 1))
                    if isinstance(i, int) and i == 3:
                        dve.wait_ge(filled, 16 * (E * CAP // P))
                    dve.tensor_tensor(row[:, p, 0:D], of_ps[:, :], x1[:, p], ALU.add).then_inc(x2_done, 1)
                if ahead and not starting:
                    dve.wait_ge(x_loaded[pa], 16 * (ka + 1))
                    dve.bn_stats(stats[:, 0], x_in[:, pa]).then_inc(ln_stats[0], 1)
                if back2:
                    dve.wait_ge(x2_done, i - 1)
                    norm_stats(2, i - 2, row[:, p, 0:D], row[:, p, D:D + 2])
                if ahead and not starting:
                    alone(dve, ln_stats[0], i + 2)
                    dve.bn_aggr(mv[:, 0], stats[:, 0]).then_inc(ln_mv[0], 1)
                if back1:
                    lo(flat(x2_t, 1), tr_a[:, :], flat(x2_t, 0), x2_hi, i, x2_lo)
                if cur:
                    dve.wait_ge(s_done, i + 1)
                    dve.reduce_max(s_max, scores_ps[:, :], AX_X).then_inc(s_maxed, 1)
                    dve.wait_ge(s_maxed, i + 1)
                    dve.wait_ge(pb_done, i + 1)
                    dve.scalar_tensor_tensor(out=s_max_b, in0=small_ps[:, PB:PB + 1], scalar=1.0 / WS,
                                             in1=s_max, op0=ALU.mult, op1=ALU.add).then_inc(s_biased, 1)
                    dve.wait_ge(s_biased, i + 1)
                    dve.scalar_tensor_tensor(out=s_shift, in0=small_ps[:, PB:PB + 1], scalar=1.0 / WS,
                                             in1=s_max_b, op0=ALU.mult, op1=ALU.subtract).then_inc(s_shifted, 1)
                if starting:
                    normalise(0, 0, x_in[:, 0], mv[:, 0], hat13[:])
                    proj_low(0)
                    dve.wait_ge(small_hi, 2)
                    dve.scalar_tensor_tensor(out=b_split[:, 1], in0=b_raw[:], scalar=WS, in1=b_split[:, 0],
                                             op0=ALU.mult, op1=ALU.subtract)
                    dve.scalar_tensor_tensor(out=wg_split[:, 1], in0=wg_raw[:], scalar=WS, in1=wg_split[:, 0],
                                             op0=ALU.mult, op1=ALU.subtract).then_inc(small_lo, 1)
                context_low(0)
                context_low(1)
                if cur:
                    lo(flat(probs_t, 1), tr_a[:, :], flat(probs_t, 0), pt_hi, i + 1, pt_lo)
                    dve.wait_ge(p_exp, i + 1)
                    dve.reciprocal(rden, den).then_inc(rden_ready, 1)
                context_low(2)
                if cur:
                    dve.wait_ge(rden_ready, i + 1)
                    dve.tensor_scalar(rden, rden, 1.0 / WS, None, ALU.mult).then_inc(rden_scaled, 1)
                context_low(3)
                if back2:
                    after(dve, p_tr, i + 1 if ahead else TILES)
                    normalise(2, i - 2, row[:, p, 0:D], row[:, p, D:D + 2], hat13[:])
                context_low(4)
                if back1:
                    dve.wait_ge(q_cast, i)
                    after(dve, st_done, i - 1)
                    dve.tensor_tensor(qk_rot[:, 0, 0:half], qk[:, 0, half:D], sin[:, 0:half], ALU.mult)
                    dve.tensor_tensor(qk_rot[:, 0, half:D], qk[:, 0, 0:half], sin[:, half:D], ALU.mult).then_inc(rope_sin, 1)
                context_low(5)
                if back2:
                    lo(flat(x3_t, 1), tr_b[:, :], flat(x3_t, 0), x3_hi, i - 1, x3_lo)
                if back1:
                    dve.wait_ge(k_cast, i)
                    dve.tensor_tensor(qk_rot[:, 1, 0:half], qk[:, 1, half:D], sin[:, 0:half], ALU.mult)
                    dve.tensor_tensor(qk_rot[:, 1, half:D], qk[:, 1, 0:half], sin[:, half:D], ALU.mult).then_inc(rope_sin, 1)
                    dve.wait_ge(rope_sin, 2 * i)
                    dve.tensor_tensor(qk[:, 0], qk[:, 0], cos, ALU.mult)
                    dve.tensor_tensor(qk[:, 1], qk[:, 1], cos, ALU.mult).then_inc(rope_cos, 1)
                if ahead and not starting:
                    if back2:
                        dve.wait_ge(x3_tr, i - 1)
                    else:
                        dve.wait_ge(p_tr, i + 1)
                    normalise(0, i + 1, x_in[:, pa], mv[:, 0], hat13[:])
                if back1:
                    dve.wait_ge(rope_cos, i)
                    dve.tensor_tensor(qk_rot[:, :, :], qk[:, :, :], qk_rot[:, :, :], ALU.add).then_inc(roped, 1)
                if starting:
                    lo(flat(p_t, 1), tr_b[:, :], flat(p_t, 0), p_hi, 1, p_lo)
                context_low(6)
                if back2:
                    dve.wait_ge(logits_mm, i - 1)
                    dve.scalar_tensor_tensor(out=logits[:], in0=q_ps[:, RT:RT + E], scalar=1.0 / WS,
                                             in1=bg_full[:], op0=ALU.mult, op1=ALU.add).then_inc(logits_done, 1)
                context_low(7)
                if back2:
                    dve.wait_ge(logits_done, i - 1)
                    dve.reduce_max(l_max, logits[:], AX_X).then_inc(l_maxed, 1)
                if cur:
                    lo(flat(att_t, 1), ua_ps[:, :], flat(att_t, 0), att_hi, i + 1, att_lo)
                if back2:
                    dve.wait_ge(l_maxed, i - 1)
                    dve.tensor_scalar(l_neg, l_max, -1.0, None, ALU.mult).then_inc(l_negated, 1)
                    dve.scalar_tensor_tensor(out=cand[:], in0=logits[:], scalar=l_max, in1=desc,
                                             op0=ALU.is_equal, op1=ALU.mult).then_inc(cand_done, 1)
                if ahead and not starting:
                    lo(flat(p_t, 1), tr_b[:, :], flat(p_t, 0), p_hi, i + 2, p_lo)
                if back2:
                    dve.wait_ge(cand_done, i - 1)
                    dve.reduce_max(rank, cand[:], AX_X).then_inc(rank_done, 1)
                if back1:
                    dve.wait_ge(st_done, i)
                    after(dve, exp_done, i - 1)
                    dve.scalar_tensor_tensor(out=masked[:], in0=k_ps[:, 0:P], scalar=float(D) ** -0.5,
                                             in1=mask, op0=ALU.mult, op1=ALU.add).then_inc(masked_done, 1)
                if back2:
                    dve.wait_ge(rank_done, i - 1)
                    dve.tensor_scalar(onehot[:], desc, rank, None, ALU.is_equal).then_inc(onehot_done, 1)
                    dve.tensor_scalar(base, rank, -float(CAP), float(E * CAP), ALU.mult, ALU.add
                                      ).then_inc(base_done, 1)
                    dve.wait_ge(token_next, i - 1)
                    dve.tensor_copy(row[:, p, D + 3:D + 4].bitcast(I32), token[:]).then_inc(token_written, 1)
                    dve.wait_ge(l_exped, i - 1)
                    dve.reciprocal(row[:, p, D + 2:D + 3], l_sum)
                    dve.wait_ge(token_written, i - 1)
                    dve.tensor_scalar(token[:], token[:], float(P), None, ALU.add).then_inc(token_next, 1)
                if cur:
                    dve.wait_ge(out_done, i + 1)
                    dve.wait_ge(rden_scaled, i + 1)
                    dve.scalar_tensor_tensor(out=x1[:, p], in0=of_ps[:, :], scalar=rden, in1=b_full[:],
                                             op0=ALU.mult, op1=ALU.add).then_inc(pre_done, 1)
                    dve.wait_ge(pre_done, i + 1)
                    dve.scalar_tensor_tensor(out=x1[:, p], in0=x1[:, p], scalar=0.0, in1=x_in[:, p],
                                             op0=ALU.max, op1=ALU.add).then_inc(x1_done, 1)
                    dve.wait_ge(x1_done, i + 1)
                    norm_stats(1, i, x1[:, p], mv[:, 1])
                    dve.wait_ge(ln_mv[1], i + 1)
                    rstd(dve, 1, i, mv[:, 1])
                    dve.wait_ge(pt_tr, i + 1)
                    normalise(1, i, x1[:, p], mv[:, 1], x2_hat[:])
                if ahead:
                    lo(flat(u_t, 1), ua_ps[:, :], flat(u_t, 0), u_hi, i + 2, u_lo, scale=1.0 / WS)
                if back2:
                    dve.wait_ge(px_done, i - 1)
                    dve.tensor_tensor_reduce(px_prod[:], q_ps[:, PX:PX + E], onehot[:], 1.0, 0.0,
                                             ALU.mult, ALU.add, pos).then_inc(pos_done, 1)
                    dve.tensor_tensor(carry[:], carry[:], onehot[:], ALU.add).then_inc(carry_done, 1)
                    dve.wait_ge(pos_done, i - 1)
                    dve.tensor_scalar(over, pos, float(CAP), float(SKIP), ALU.is_ge, ALU.mult
                                      ).then_inc(over_done, 1)
                    dve.wait_ge(base_done, i - 1)
                    dve.tensor_tensor(slot_f[:], pos, base, ALU.add).then_inc(slot_f_done, 1)
                    dve.wait_ge(slot_f_done, i - 1)
                    dve.wait_ge(over_done, i - 1)
                    dve.tensor_tensor(slot[:, p], slot_f[:], over, ALU.add).then_inc(row_ready, 1)
                if starting:
                    proj_low(1)
                    proj_low(2)
                    proj_low(3)
                if isinstance(i, int) and i == 3:
                    for kk in range(SPLIT_SLOTS):
                        chunk_low(0, kk)

            def chunk_low(e, kk):
                if kk not in LO_ON_POOL:
                    w = w_split[kk % SPLIT_SLOTS]
                    lo(w[:, 1], raw[kk], w[:, 0], w_hi[kk], e + 1, w_lo[kk], scale=WS)

            each_step(dve, step)

            def rows_hat(e, k, p):
                dve.wait_ge(e_loaded[p], 16 * (k + 1))
                after(dve, e_tr, e)
                dve.tensor_scalar(e_hat, e_row[p][:, 0:D], e_row[p][:, D:D + 1], e_row[p][:, D + 1:D + 2],
                                  ALU.subtract, ALU.mult).then_inc(e_norm, 1)
                dve.tensor_scalar(gate_e[p], e_row[p][:, D + 2:D + 3], 1.0 / WS, None, ALU.mult).then_inc(gate_done, 1)

            def rows_lo(e):
                lo(flat(e_t, 1), tr_a[:, :], flat(e_t, 0), e_hi, e + 1, e_lo)
                dve.wait_ge(e_idx, e + 1)
                dve.tensor_scalar(is_e, p_index, e_index[:, 0:1], None, ALU.is_equal).then_inc(e_sel_steps, 1)
                dve.wait_ge(e_sel_steps, e + 1)
                dve.tensor_scalar(sel, ones16, is_e[:, 0:1], None, ALU.mult).then_inc(e_sel, 1)
                dve.tensor_scalar(e_index, e_index, 1.0, None, ALU.add).then_inc(e_idx, 1)

            def expert(e, k, p, last):
                kn, pn = neighbour(k, p, 1)
                for kk, (which, hb) in enumerate(ORDER):
                    if which == 1:
                        n = 4 * e + hb
                        dve.wait_ge(h_relu, n + 1)
                        dve.tensor_copy(hid_split[hb][:, 0], hid[hb % 2]).then_inc(h_hi, 1)
                        lo(hid_split[hb][:, 1], hid[hb % 2], hid_split[hb][:, 0], h_hi, n + 1, h_lo)
                    if kk == CHUNKS - 1:
                        dve.wait_ge(w_used, CHUNKS * (e + 1))
                        dve.wait_ge(gate_done, e + 1)
                        after(dve, out_scat[p], 16 * k)
                        dve.scalar_tensor_tensor(out=o_row[p], in0=y_ps[:, :], scalar=gate_e[p][:, 0:1],
                                                 in1=e_row[p][:, 0:D], op0=ALU.mult, op1=ALU.add).then_inc(y_out, 1)
                    if kk < SPLIT_SLOTS or not last:
                        chunk_low(*later(e, kk))
                    if kk == 3 and not last:
                        rows_hat(e + 1, kn, pn)
                    if kk == 6 and not last:
                        rows_lo(e + 1)

            dve.wait_ge(k_done, TILES)
            dve.memset(b2_raw, 0.0).then_inc(b2_zero, 1)
            dve.memset(e_index, 0.0).then_inc(e_idx, 1)
            rows_hat(0, 0, 0)
            rows_lo(0)
            dve.wait_ge(b2_hi, 1)
            dve.scalar_tensor_tensor(out=b2_split[:, 1], in0=b2_raw, scalar=WS, in1=b2_split[:, 0],
                                     op0=ALU.mult, op1=ALU.subtract).then_inc(b2_lo, 1)
            each_expert(dve, expert)

        @block.gpsimd
        def _(pool):
            pool.memset(fill[:, 0:D + 3], 0.0).then_inc(begun, 1)
            pool.memset(fill[:, D + 3:D + 4].bitcast(I32), SKIP).then_inc(begun, 1)

            def step(i, k, p, ahead, cur, back1, back2):
                if back2:
                    alone(pool, ln_mv[2], i - 1)
                    rstd(pool, 2, i - 2, row[:, p, D:D + 2])
                if ahead:
                    alone(pool, ln_mv[0], i + 2)
                    rstd(pool, 0, i + 1, mv[:, 0])
                if back2:
                    pool.dma_start(out[bass.ds((i - 2) * P, P), :], row[:, p, 0:D]).then_inc(base_out[p], 16)
                if ahead:
                    for j in range(2):
                        alone(pool, nat_hi, 2 * (i + 1) + j + 1)
                        pool.tensor_tensor(ctx_nat[:, j, 1], ctx_raw[j], ctx_nat[:, j, 0], ALU.subtract
                                           ).then_inc(nat_lo, 1)
                if back2:
                    alone(pool, row_ready, i - 1)
                    alone(pool, ln_step[2], RSQRT_STEPS * (i - 1))
                    if isinstance(i, int) and i == 2:
                        pool.wait_ge(filled, 16 * (E * CAP // P))
                    alone(pool, scattered[1 - p], 16 * neighbour(k, p, -1)[0])
                    pool.indirect_dma_start(
                        out=slot_table, out_offset=bass.IndirectOffsetOnAxis(ap=slot[:, p].bitcast(U32), axis=0),
                        in_=row[:, p, :], in_offset=None, bounds_check=E * CAP - 1, oob_is_err=False,
                    ).then_inc(scattered[p], 16)
                if isinstance(i, int) and i == 3:
                    scale_chunk(0, LO_ON_POOL[0])
                    chunk_low(0, LO_ON_POOL[0])

            def scale_chunk(e, kk):
                alone(pool, w_in[kk], 16 * (e + 1))
                pool.tensor_scalar(raw[kk], raw[kk], WS, 1.0, ALU.mult, ALU.mult).then_inc(w_scaled[kk], 1)

            def chunk_low(e, kk):
                w = w_split[kk % SPLIT_SLOTS]
                alone(pool, w_hi[kk], e + 1)
                pool.tensor_tensor(w[:, 1], raw[kk], w[:, 0], ALU.subtract).then_inc(w_lo[kk], 1)

            each_step(pool, step)

            def scatter_out(e, k, p):
                alone(pool, y_out, e + 1)
                alone(pool, out_scat[1 - p], 16 * (neighbour(k, p, -1)[0] + 1))
                pool.indirect_dma_start(
                    out=out, out_offset=bass.IndirectOffsetOnAxis(ap=e_row[p][:, D + 3:D + 4].bitcast(U32), axis=0),
                    in_=o_row[p], in_offset=None, bounds_check=TOK - 1, oob_is_err=False,
                ).then_inc(out_scat[p], 16)

            def expert(e, k, p, last):
                kb, pb = neighbour(k, p, -1)
                for kk in range(CHUNKS):
                    if kk < SPLIT_SLOTS or not last:
                        el, kl = later(e, kk)
                        if kl in LO_ON_POOL:
                            m = LO_ON_POOL.index(kl) + 1
                            if m < len(LO_ON_POOL):
                                scale_chunk(el, LO_ON_POOL[m])
                            elif not last:
                                scale_chunk(el + 1, LO_ON_POOL[0])
                            chunk_low(el, kl)
                    if kk == 1 and not (isinstance(e, int) and e == 0):
                        scatter_out(e - 1, kb, pb)

            scale_chunk(0, LO_ON_POOL[1])
            for n in range(2):
                pool.wait_ge(base_out[n], 16 * (TILES // 2))
            each_expert(pool, expert)
            scatter_out(E - 1, E // 2 - 1, 1)
            for n in range(2):
                pool.wait_ge(out_scat[n], 16 * (E // 2))


def tables():
    k, q = np.arange(P)[:, None], np.arange(P)[None, :]
    mask = np.where((k // L == q // L) & (k <= q), 0.0, NEG).astype(np.float32)
    desc = np.broadcast_to(E - np.arange(E, dtype=np.float32), (P, E))
    f32 = np.concatenate([np.eye(P, dtype=np.float32), mask, desc, np.arange(P, dtype=np.float32)[:, None]], 1)
    inv = (np.float32(ROPE_BASE) ** (-np.arange(0, D, 2, dtype=np.float32) / np.float32(D))).astype(np.float32)
    angle = np.arange(L, dtype=np.float32)[None, :] * inv[:, None]
    parts = []
    for f, sign in ((np.cos, (1, 1)), (np.sin, (-1, 1))):
        v = f(angle).astype(np.float32).reshape(C // 2, P, L).transpose(1, 0, 2)
        v = np.concatenate([sign[0] * v, sign[1] * v], 1)
        parts.append(np.concatenate([v, v], 2).reshape(P, D))
    parts += [(k < q).astype(np.float32), np.ones((P, P), np.float32)]
    return np.ascontiguousarray(f32), np.concatenate(parts, 1)


def kernel(**inputs):
    import ml_dtypes
    from concourse import bacc
    from concourse.bass_utils import run_bass_kernel_spmd

    def a(name):
        return np.asarray(inputs[name])

    f32, f16 = tables()
    w = a("L0_xattn_W")
    ctx = a("ctx_1024")
    arrays = {
        "x": a("x").reshape(TOK, D),
        "ctx": ctx,
        "ctx_tr": ctx.reshape(B, P, 4, C, P).transpose(0, 4, 3, 2, 1).reshape(B, P, C, LQ),
        "w_nat": w,
        "w_t": w.T,
        "wq_t": a("L0_attn_Wq").T,
        "wk_t": a("L0_attn_Wk").T,
        "b_row": a("L0_xattn_b"),
        "b_col": a("L0_xattn_b").reshape(C, P).T,
        "fc1_w": a("L0_attn_fc1_w").reshape(INNER),
        "fc1_b": a("L0_attn_fc1_b").reshape(INNER, 1),
        "fc2_t": a("L0_attn_fc2_w").T,
        "fc2_b": a("L0_attn_fc2_b").reshape(1, D),
        "wg": a("L0_ffn_Wg"),
        "bg": a("L0_ffn_bg"),
        "w1": a("L0_ffn_W1").reshape(E, C, P, HB, D).transpose(0, 3, 2, 1, 4),
        "b1": a("L0_ffn_b1").reshape(E, H // P, P).transpose(0, 2, 1),
        "w2": a("L0_ffn_W2").reshape(E, HB, C, P, D).transpose(0, 1, 3, 2, 4),
        "b2": a("L0_ffn_b2"),
        "consts": f32,
        "consts16": f16.astype(ml_dtypes.bfloat16),
    }
    arrays = {n: np.ascontiguousarray(v) for n, v in arrays.items()}
    nc = bacc.Bacc("TRN2", target_bir_lowering=False, num_devices=1)
    args = {n: nc.dram_tensor(n, v.shape, mybir.dt.from_np(v.dtype), kind="ExternalInput").ap()
            for n, v in arrays.items()}
    out = nc.dram_tensor("out", [TOK, D], F32, kind="ExternalOutput").ap()
    program(nc, out=out, **args)
    r = run_bass_kernel_spmd(nc, [arrays], core_ids=[0])
    return r.results[0]["out"].reshape(B, L, D)
```

```python
from contextlib import ExitStack

import numpy as np

import concourse.bass as bass
from concourse import mybir

F32 = mybir.dt.float32
F16 = mybir.dt.float16
BF16 = mybir.dt.bfloat16
I32 = mybir.dt.int32
U32 = mybir.dt.uint32
ALU = mybir.AluOpType
ACT = mybir.ActivationFunctionType
AX_X = mybir.AxisListType.X

P = 128
B = 32
L = 64
D = 512
LQ = 512
C = D // P
E = 16
H = 2048
INNER = 16
TOK = B * L
TILES = TOK // P
CAP = -(-TOK // E)
HB = H // D
ROPE_BASE = 32.0
EPS = 1e-5
WS = 64.0
ROW = D + 4
SKIP = 1 << 20
RSQRT_MAGIC = 0x5F1FFFF9
RSQRT_FACTOR, RSQRT_TERM = 0.703952253, 2.38924456
RSQRT_STEPS = 9
NEG = -1e30

ORDER = [(1, 0), (1, 1), (1, 2), (2, 0), (1, 3), (2, 1), (2, 2), (2, 3)]
CHUNKS = len(ORDER)
CTX_ON_DVE = 6
POOL_LOS = 8 - CTX_ON_DVE + 2
LO_ON_POOL = (2, 6)
LO_ON_DVE = [kk for kk in range(CHUNKS) if kk not in LO_ON_POOL]
RESTS_FIRST = (10, 18, 16)
RESTS = ((9, 2, 0, 0, 5, 6, 0), (4, 2, 18, 11, 5, 38, 7))

PB, H1 = 0, 128
RT, PX = 0, 16


def program(nc, x, ctx, ctx_tr, w_nat, w_t, wq_t, wk_t, b_row, b_col, fc1_w, fc1_b, fc2_t, fc2_b, wg, bg,
            w1, b1, w2, b2, consts, consts16, out):
    with ExitStack() as stack:
        def sb(name, shape, dt):
            return stack.enter_context(nc.sbuf_tensor(name, shape, dt))

        def sem(name):
            return stack.enter_context(nc.semaphore(name))

        def bank(name):
            return stack.enter_context(nc.psum_tensor(name, [P, 512], F32))

        def after(eng, semaphore, count):
            if not isinstance(count, int) or count > 0:
                eng.wait_ge(semaphore, count)

        def alone(eng, semaphore, count):
            after(eng, semaphore, count)
            if not isinstance(count, int):
                eng.sem_inc(passed, 1)

        slot_table = nc.dram_tensor("slot_table", [E * CAP, ROW], F32, kind="Internal").ap()

        raw_low = sb("raw_weights_0_3", [P, 4, 4, D], F32)
        arena = sb("raw_context_then_raw_weights_4_7", [P, 4, 4, D], F32)
        split_arena = sb("raw_projections_then_split_chunks_0_3", [P, 4, 4, D], F32)
        proj_arena = sb("projections_then_expert_tiles", [P, 4, 4 * D], F32)
        ctx_t = sb("context_transposed", [P, 2, 2, C, LQ], F16)
        ctx_nat = sb("context_natural", [P, 2, 2, C, D], F16)

        raw = [raw_low[:, n] for n in range(4)] + [arena[:, n] for n in range(4)]
        ctx_t_raw = [arena[:, j] for j in range(2)]
        ctx_raw = [arena[:, 2 + j] for j in range(2)]
        proj_raw = [split_arena[:, n] for n in range(4)]
        w_split = [split_arena[:, n].rearrange("p c d -> p (c d)").bitcast(F16)
                   .rearrange("p (s c d) -> p s c d", s=2, c=4) for n in range(4)]
        w_split += [ctx_t[:, j] for j in range(2)] + [ctx_nat[:, j] for j in range(2)]
        proj = [proj_arena[:, n].bitcast(F16).rearrange("p (s c d) -> p s c d", s=2, c=4) for n in range(4)]
        W_U, W_O, W_Q, W_K = proj

        x_ahead = sb("x_for_first_norm", [P, D], F32)
        x_res = sb("x_to_add", [P, D], F32)
        hat = sb("normalised", [P, D], F32)
        p_t = sb("p_transposed", [P, 2, C, P], F16)
        u_t = sb("u_transposed", [P, 2, C, P], F16)
        probs = sb("probs", [P, LQ], F32)
        probs_t = sb("probs_transposed", [P, 2, C, P], F16)
        att_t = sb("att_transposed", [P, 2, C, P], F16)
        x1 = sb("x1", [P, 2, D], F32)
        x2_t = sb("x2_transposed", [P, 2, C, P], F16)
        qk = sb("qk", [P, 2, D], BF16)
        qk_rot = sb("qk_rotated", [P, 2, D], BF16)
        masked = sb("masked_scores", [P, P], F32)
        exp_t = sb("exp_scores", [P, P], F32)
        inner = sb("inner", [P, P], F32)
        row = sb("rows_for_slots", [P, 2, ROW], F32)
        fill = row[:, 1]
        x3_t = sb("x3_transposed", [P, 2, C, P], F16)

        cst = sb("tables_f32", [P, 2 * P + E + 1], F32)
        ident, mask = cst[:, 0:P], cst[:, P:2 * P]
        desc, p_index = cst[:, 2 * P:2 * P + E], cst[:, 2 * P + E:2 * P + E + 1]
        cst16 = sb("tables_bf16", [P, 2 * D + 2 * P], BF16)
        cos, sin = cst16[:, 0:D], cst16[:, D:2 * D]
        before, ones16 = cst16[:, 2 * D:2 * D + P], cst16[:, 2 * D + P:2 * D + 2 * P]
        b_full = sb("b_on_all_partitions", [P, D], F32)
        b_raw = sb("b_column", [P, C], F32)
        b_split = sb("b_column_split", [P, 2, C], F16)
        fc1_rows = sb("fc1_on_all_rows", [P, P], F32)
        fc1_bias = sb("fc1_bias", [P, 1], F32)
        fc2 = sb("fc2", [P, D], F32)
        wg_raw = sb("wg_raw", [P, C, E], F32)
        wg_split = sb("wg_split", [P, 2, C, E], F16)
        bg_full = sb("bg_on_all_partitions", [P, E], F32)

        stats = sb("stats", [P, 3, 6], F32)
        mv = sb("mean_var", [P, 2, 2], F32)
        newton = sb("newton", [P, 3, 3], F32)
        minus_mean = sb("minus_mean_over_std", [P, 3], F32)
        small = sb("small", [P, 12], F32)
        (s_max, s_max_b, s_shift, den, rden, l_max, l_neg, l_sum, rank, pos, base, over) = (
            small[:, n:n + 1] for n in range(12))
        slot_f = sb("slot_before_capacity", [P, 1], F32)
        logits = sb("logits", [P, E], F32)
        l_exp = sb("logit_exp", [P, E], F32)
        cand = sb("candidates", [P, E], F32)
        onehot = sb("onehot", [P, E], BF16)
        carry = sb("tokens_so_far", [P, E], BF16)
        px_prod = sb("position_product", [P, E], F32)
        slot = sb("slot", [P, 2, 1], I32)
        token = sb("token", [P, 1], F32)

        ffn = proj_arena[:, :].rearrange("p a b -> p (a b)")
        taken = [0]

        def carve(n):
            at = taken[0]
            taken[0] = at + n
            assert taken[0] <= 16 * D
            return ffn[:, at:at + n]

        e_row = [carve(ROW) for _ in range(2)]
        e_hat = carve(D)
        e_t = carve(D).bitcast(F16).rearrange("p (s c n) -> p s c n", s=2, c=C)
        hid = [carve(D) for _ in range(2)]
        hid_split = [carve(D).bitcast(F16).rearrange("p (s n) -> p s n", s=2) for _ in range(HB)]
        o_row = [carve(D) for _ in range(2)]
        b2_raw = carve(D)
        b2_split = carve(D).bitcast(F16).rearrange("p (s n) -> p s n", s=2)
        b1_e = [carve(H // P) for _ in range(2)]
        gate_e = [carve(1) for _ in range(2)]
        token_next_e = [carve(1).bitcast(U32) for _ in range(2)]
        token_e = [carve(1).bitcast(U32) for _ in range(2)]
        e_x = [x1[:, p] for p in range(2)]
        sel = carve(P // 2).bitcast(F16)
        is_e = carve(1)
        e_index = carve(1)

        scores_ps = bank("scores_ps")
        tr_a = bank("transposes_a_ps")
        tr_b = bank("transposes_b_ps")
        ua_ps = bank("u_att_ps")
        q_ps = bank("q_routing_ps")
        k_ps = bank("k_self_scores_ps")
        of_ps = bank("out_fc2_ps")
        small_ps = bank("small_ps")
        hid_ps = [q_ps, k_ps]
        y_ps = of_ps

        passed = sem("waits_passed")
        consts_in = sem("consts_in")
        smalls_in = sem("small_inputs_in")
        begun = sem("begun")
        proj_in = [sem(f"proj_in{n}") for n in range(4)]
        proj_hi = sem("proj_hi")
        proj_lo = sem("proj_lo")
        small_hi = sem("small_hi")
        small_lo = sem("small_lo")
        zeroed = sem("zeroed")
        padded = sem("padded")
        filled = sem("table_filled")
        x_ahead_in = sem("x_for_first_norm_in")
        x_res_in = sem("x_to_add_in")
        b_in = sem("b_and_wg_in")
        ctx_loaded = [sem(f"ctx_loaded{n}") for n in range(2)]
        ctx_t_loaded = [sem(f"ctx_t_loaded{n}") for n in range(2)]
        ln_stats = [sem(f"ln{n}_stats") for n in range(3)]
        ln_mv = [sem(f"ln{n}_mean_var") for n in range(3)]
        ln_step = [sem(f"ln{n}_rsqrt_steps") for n in range(3)]
        ln_shift = {n: sem(f"ln{n}_shift") for n in (0, 2)}
        ln_hat = [sem(f"ln{n}_normalised") for n in range(3)]
        p_tr = sem("p_transposes")
        p_hi = sem("p_hi")
        p_lo = sem("p_lo")
        u_done = sem("u_done")
        u_hi = sem("u_hi")
        u_lo = sem("u_lo")
        pb_done = sem("pb_done")
        ctx_hi = sem("ctx_t_hi_halves")
        ctx_lo = sem("ctx_t_lo_quarters_on_dve")
        nat_hi = sem("ctx_natural_hi_halves")
        pool_lo = sem("ctx_lo_on_pool")
        s_done = sem("scores_done")
        shift_steps = sem("scores_shift_steps")
        s_shifted = sem("scores_shift")
        p_exp = sem("probs_exp")
        rden_steps = sem("rden_steps")
        pt_tr = sem("probs_transposes")
        pt_hi = sem("probs_hi")
        pt_lo = sem("probs_lo")
        att_done = sem("att_done")
        att_hi = sem("att_hi")
        att_lo = sem("att_lo")
        out_done = sem("out_done")
        pre_done = sem("pre_relu_done")
        b2_in, b2_zero, b2_hi, b2_lo = (sem(n) for n in ("b2_in", "b2_zeroed", "b2_hi", "b2_lo"))
        x1_done = sem("x1_done")
        x2_tr = sem("x2_transposes")
        x2_hi = sem("x2_hi")
        x2_lo = sem("x2_lo")
        q_done = sem("q_done")
        k_done = sem("k_done")
        q_cast = sem("q_cast")
        k_cast = sem("k_cast")
        rope_sin = sem("rope_sin")
        rope_cos = sem("rope_cos")
        roped = sem("roped")
        st_done = sem("st_done")
        masked_done = sem("masked_done")
        exp_done = sem("exp_done")
        h1_done = sem("h1_done")
        inner_done = sem("inner_done")
        fc2_done = sem("fc2_done")
        x2_done = sem("x2_done")
        x3_tr = sem("x3_transposes")
        x3_hi = sem("x3_hi")
        x3_lo = sem("x3_lo")
        logits_mm = sem("logits_mm")
        logits_done = sem("logits_done")
        l_maxed = sem("logits_maxed")
        l_negated = sem("logits_max_negated")
        l_exped = sem("logits_exp")
        cand_done = sem("candidates_done")
        rank_done = sem("rank_done")
        onehot_done = sem("onehot_done")
        px_done = sem("prefix_done")
        carry_done = sem("carry_done")
        pos_done = sem("position_done")
        base_done = sem("first_slot_done")
        over_done = sem("over_done")
        slot_f_done = sem("slot_f_done")
        row_ready = sem("row_ready")
        token_written = sem("token_written")
        token_next = sem("token_next")
        base_out = [sem(f"x2_stored{n}") for n in range(2)]
        scattered = [sem(f"row_scattered{n}") for n in range(2)]

        w_in = [sem(f"w_chunk_loaded{n}") for n in range(CHUNKS)]
        w_scaled = [sem(f"w_chunk_scaled{n}") for n in range(CHUNKS)]
        w_hi = [sem(f"w_chunk_hi{n}") for n in range(CHUNKS)]
        w_lo = [sem(f"w_chunk_lo{n}") for n in range(CHUNKS)]
        w_used = sem("w_chunks_used")
        e_loaded = [sem(f"expert_rows_loaded{n}") for n in range(2)]
        b1_loaded = [sem(f"b1_loaded{n}") for n in range(2)]
        e_norm = sem("expert_rows_normalised")
        e_tr = sem("expert_transposes")
        e_hi = sem("expert_rows_hi")
        e_lo = sem("expert_rows_lo")
        e_idx = sem("expert_index")
        e_sel = sem("expert_selected")
        e_sel_steps = sem("expert_select_steps")
        gate_done = sem("gate_done")
        h_relu = sem("hidden_blocks_relu")
        h_hi = sem("hidden_blocks_hi")
        h_lo = sem("hidden_blocks_lo")
        y_out = sem("y_out")
        out_scat = [sem(f"out_scattered{n}") for n in range(2)]

        block = stack.enter_context(nc.Block())

        def each_step(eng, step):
            for i in range(-1, 4):
                step(i, i // 2, i % 2, True, True, i >= 0, i >= 1, i >= 2)
            with eng.Fori(2, TILES // 2 - 1) as k:
                for p in range(2):
                    step(2 * k + p, k, p, True, True, True, True, True)
            for i in range(TILES - 2, TILES + 2):
                step(i, i // 2, i % 2, False, i < TILES - 1, i < TILES, i <= TILES, True)

        def each_expert(eng, expert):
            for e in range(6):
                expert(e, e // 2, e % 2, e)
            with eng.Fori(3, E // 2 - 1) as k:
                for p in range(2):
                    expert(2 * k + p, k, p, 6)
            for e in range(E - 2, E):
                expert(e, e // 2, e % 2, e)

        def split_ahead(turn):
            return CHUNKS if turn < 4 else CHUNKS // 2

        def chunk_to_split(e, kk, turn):
            n = kk + split_ahead(turn)
            if kk < split_ahead(max(turn - 1, 0)) - split_ahead(turn) or (turn == E - 1 and n >= CHUNKS):
                return None
            return (e, n) if n < CHUNKS else (e + 1, n - CHUNKS)

        def on_pool(e, kk):
            return kk in LO_ON_POOL and not (isinstance(e, int) and e == E - 1 and kk >= CHUNKS // 2)

        def neighbour(k, p, d):
            return k + (p + d) // 2, (p + d) % 2

        def chunk_source(e, kk):
            which, hb = ORDER[kk]
            return (w1 if which == 1 else w2)[bass.ds(e, 1), hb].rearrange("o p c d -> (o p) c d")

        def rstd_guess(eng, n, t, moments):
            v, y = (newton[:, n, m:m + 1] for m in range(2))
            at, done = RSQRT_STEPS * t, ln_step[n]
            eng.tensor_scalar(v, moments[:, 1:2], EPS, 1.0, ALU.add, ALU.mult).then_inc(done, 1)
            alone(eng, done, at + 1)
            eng.tensor_scalar(y.bitcast(I32), v.bitcast(I32), -0.5, float(RSQRT_MAGIC), ALU.mult, ALU.add
                              ).then_inc(done, 1)

        def rstd_newton(eng, n, t):
            v, y, h = (newton[:, n, m:m + 1] for m in range(3))
            at, done = RSQRT_STEPS * t, ln_step[n]
            alone(eng, done, at + 2)
            eng.tensor_scalar(h, y, v, y, ALU.mult, ALU.mult).then_inc(done, 1)
            alone(eng, done, at + 3)
            eng.tensor_scalar(h, h, -RSQRT_FACTOR, RSQRT_FACTOR * RSQRT_TERM, ALU.mult, ALU.add).then_inc(done, 1)
            alone(eng, done, at + 4)
            eng.tensor_tensor(y, y, h, ALU.mult).then_inc(done, 1)

        def rstd_cubic(eng, n, t, moments):
            v, y, h = (newton[:, n, m:m + 1] for m in range(3))
            at, done = RSQRT_STEPS * t, ln_step[n]
            alone(eng, done, at + 5)
            eng.tensor_scalar(h, y, v, y, ALU.mult, ALU.mult).then_inc(done, 1)
            alone(eng, done, at + 6)
            eng.tensor_scalar(v, h, 0.375, -1.25, ALU.mult, ALU.add).then_inc(done, 1)
            alone(eng, done, at + 7)
            eng.tensor_scalar(v, v, h, 1.875, ALU.mult, ALU.add).then_inc(done, 1)
            alone(eng, done, at + 8)
            eng.tensor_tensor(moments[:, 1:2], y, v, ALU.mult).then_inc(done, 1)

        @block.sync
        def _(sp):
            def load_context(t, transposed):
                for j in range(2):
                    if transposed:
                        alone(sp, ctx_lo, CTX_ON_DVE * (t - 1) + (4, CTX_ON_DVE)[j])
                        if j == 1:
                            alone(sp, pool_lo, POOL_LOS * t - 2)
                        sp.dma_start(ctx_t_raw[j], ctx_tr[bass.ds(2 * t + j, 1)].rearrange("o p c d -> (o p) c d")
                                     ).then_inc(ctx_t_loaded[j], 16)
                    else:
                        alone(sp, pool_lo, POOL_LOS * t - 1 + j)
                        sp.dma_start(ctx_raw[j], ctx[bass.ds(2 * t + j, 1)].rearrange("o (p c) d -> (o p) c d", c=4)
                                     ).then_inc(ctx_loaded[j], 16)

            def load_proj(n):
                w = (w_nat, w_t, wq_t, wk_t)[n]
                sp.dma_start(proj_raw[n], w.rearrange("(c p) d -> p c d", p=P)).then_inc(proj_in[n], 16)

            def load_ahead(t):
                sp.wait_ge(ln_hat[0], t)
                sp.dma_start(x_ahead[:], x[bass.ds(t * P, P), :]).then_inc(x_ahead_in, 16)

            sp.dma_start(x_ahead[:], x[0:P, :]).then_inc(x_ahead_in, 16)
            load_proj(0)
            sp.dma_start(cst[:], consts).then_inc(consts_in, 16)
            sp.dma_start(ctx_t_raw[0], ctx_tr[0]).then_inc(ctx_t_loaded[0], 16)
            sp.dma_start(b_raw[:], b_col).then_inc(b_in, 16)
            sp.dma_start(wg_raw[:], wg.rearrange("(c p) e -> p c e", p=P)).then_inc(b_in, 16)
            sp.dma_start(ctx_t_raw[1], ctx_tr[1]).then_inc(ctx_t_loaded[1], 16)
            load_ahead(1)

            def load_smalls():
                load_proj(1)
                sp.dma_start(b_full[:], b_row.partition_broadcast(P)).then_inc(smalls_in, 16)
                sp.dma_start(bg_full[:], bg.partition_broadcast(P)).then_inc(smalls_in, 16)
                sp.dma_start(cst16[:], consts16).then_inc(smalls_in, 16)
                sp.wait_ge(zeroed, 3)
                sp.dma_start(fc1_rows[:, 0:INNER], fc1_w.partition_broadcast(P)).then_inc(padded, 16)
                sp.dma_start(fc1_bias[0:INNER, :], fc1_b).then_inc(padded, 16)
                sp.dma_start(fc2[0:INNER, :], fc2_t).then_inc(padded, 16)
                sp.dma_start(fc2[32:33, :], fc2_b).then_inc(padded, 16)

            def step(i, k, p, ahead2, ahead, cur, back1, back2):
                straight = isinstance(i, int)
                if ahead2 and not (straight and i < 1):
                    load_ahead(i + 2)
                if cur:
                    after(sp, x1_done, i)
                    sp.dma_start(x_res[:], x[bass.ds(i * P, P), :]).then_inc(x_res_in, 16)
                if ahead:
                    load_context(i + 1, False)
                if straight and i == TILES - 2:
                    for kk in range(4):
                        sp.dma_start(raw[kk], chunk_source(0, kk)).then_inc(w_in[kk], 16)
                if straight and i == -1:
                    load_smalls()
                if straight and i == 0:
                    load_proj(2)
                    load_proj(3)
                if straight and 0 <= i <= 2:
                    sp.wait_ge(begun, 2)
                    for n in range((0, 4, 10)[i], (4, 10, E * CAP // P)[i]):
                        sp.dma_start(slot_table[n * P:(n + 1) * P, :], fill).then_inc(filled, 16)
                if ahead2:
                    load_context(i + 2, True)
                if straight and i == -1:
                    load_ahead(2)

            each_step(sp, step)

            def load_rows(e, p):
                after(sp, gate_done, e - 1)
                sp.dma_start(e_row[p], slot_table[bass.ds(e * CAP, CAP), :]).then_inc(e_loaded[p], 16)

            def load_b1(e, p):
                after(sp, h_relu, HB * (e - 1))
                sp.dma_start(b1_e[p], b1[bass.ds(e, 1)].rearrange("o p c -> (o p) c")).then_inc(b1_loaded[p], 16)

            def load_chunk(e, kk):
                alone(sp, w_lo[kk], e)
                sp.dma_start(raw[kk], chunk_source(e, kk)).then_inc(w_in[kk], 16)

            for kk in range(4, CHUNKS):
                if kk < 6:
                    sp.wait_ge(ctx_lo, CTX_ON_DVE * (TILES - 1) + (4, CTX_ON_DVE)[kk - 4])
                if kk > 4:
                    sp.wait_ge(pool_lo, POOL_LOS * TILES + kk - 7)
                sp.dma_start(raw[kk], chunk_source(0, kk)).then_inc(w_in[kk], 16)
            for kk in range(4):
                load_chunk(1, kk)
            for n in range(2):
                sp.wait_ge(scattered[n], 16 * (TILES // 2))
            for e in range(2):
                load_rows(e, e)
                load_b1(e, e)
            sp.wait_ge(b2_zero, 1)
            sp.dma_start(b2_raw[0:E, :], b2).then_inc(b2_in, 16)
            for kk in range(4, CHUNKS):
                load_chunk(1, kk)
            with sp.Fori(1, E // 2) as k:
                for p in range(2):
                    load_rows(2 * k + p, p)
                    for kk in range(CHUNKS):
                        load_chunk(2 * k + p, kk)
                        if kk == 3:
                            load_b1(2 * k + p, p)

        @block.tensor
        def _(pe):
            def three(out_ps, left, right, first, last):
                pe.matmul(out_ps, left[0], right[0], start=first, stop=False)
                pe.matmul(out_ps, left[0], right[1], start=False, stop=False)
                return pe.matmul(out_ps, left[1], right[0], start=False, stop=last)

            def both(a, *at):
                return (a[(slice(None), 0) + at], a[(slice(None), 1) + at])

            def transpose4(dst, source):
                for c in range(C):
                    mm = pe.transpose(dst[:, c * P:(c + 1) * P], source[:, c * P:(c + 1) * P], ident)
                return mm

            def cols(c):
                return slice(c * P, (c + 1) * P)

            A = slice(None)

            def keep_clock(n):
                for _ in range(n):
                    pe.matmul(scores_ps[:, :], p_t[:, 0, 0], flat_high(p_t), start=True, stop=True)

            def flat_high(a):
                return a[:, 0].rearrange("p c n -> p (c n)")

            def score_chunks(chunks):
                for c in chunks:
                    for n, (a, b) in enumerate(((0, 0), (0, 1), (1, 0))):
                        for j in range(2):
                            mm = pe.matmul(scores_ps[j * L:(j + 1) * L, :], u_t[:, a, c, j * L:(j + 1) * L],
                                           ctx_t[:, j, b, c, :], start=(c == 0 and n == 0),
                                           stop=(c == C - 1 and n == 2))
                return mm

            def project(ps, w, ocs):
                for oc in ocs:
                    for c in range(C):
                        mm = three(ps[:, cols(oc)], both(w, c, cols(oc)), both(x2_t, c, A), c == 0, c == C - 1)
                return mm

            def step(i, k, p, ahead2, ahead, cur, back1, back2):
                straight = isinstance(i, int)

                def rest(stage):
                    if straight and i >= TILES:
                        keep_clock(RESTS[i - TILES][stage])

                if cur:
                    pe.wait_ge(u_lo, i + 1)
                    pe.wait_ge(ctx_lo, CTX_ON_DVE * (i + 1))
                    pe.wait_ge(pool_lo, POOL_LOS * (i + 1) - 2)
                    after(pe, p_exp, i)
                    score_chunks((0, 1))
                if back2:
                    pe.wait_ge(roped, i - 1)
                    for c in range(C):
                        mm = pe.matmul(k_ps[:, 0:P], qk_rot[:, 1, cols(c)], qk_rot[:, 0, cols(c)],
                                       start=(c == 0), stop=(c == C - 1))
                    mm.then_inc(st_done, 1)
                    rest(0)
                if cur:
                    score_chunks((2, 3)).then_inc(s_done, 1)
                if ahead:
                    pe.wait_ge(p_lo, i + 2)
                    after(pe, att_lo, i)
                    if straight and i == -1:
                        pe.wait_ge(proj_lo, 1)
                    for hc in range(C):
                        for c in range(C):
                            mm = three(ua_ps[:, cols(hc)], both(W_U, c, cols(hc)), both(p_t, c, A), c == 0, c == C - 1)
                    mm.then_inc(u_done, 1)
                    after(pe, s_shifted, i + 1)
                    after(pe, inner_done, i - 2)
                    if straight and i == -1:
                        pe.wait_ge(small_lo, 1)
                    for c in range(C):
                        mm = three(small_ps[:, PB:PB + 1], both(p_t, c, A), both(b_split, slice(c, c + 1)),
                                   c == 0, c == C - 1)
                    mm.then_inc(pb_done, 1)
                    if straight and i == -1:
                        keep_clock(RESTS_FIRST[1])
                if back2:
                    pe.wait_ge(exp_done, i - 1)
                    if cur:
                        pe.wait_ge(s_shifted, i + 1)
                    if straight and i == 2:
                        pe.wait_ge(padded, 16 * 4)
                    pe.matmul(small_ps[:, H1:H1 + P], fc1_rows[:], exp_t[:], start=True, stop=True).then_inc(h1_done, 1)
                    rest(1)
                if cur:
                    pe.wait_ge(p_exp, i + 1)
                    after(pe, pt_lo, i)
                    transpose4(tr_a, probs).then_inc(pt_tr, 1)
                if back2:
                    pe.wait_ge(inner_done, i - 1)
                    pe.wait_ge(pre_done, min(i, TILES) if straight else i)
                    pe.matmul(of_ps[:, :], inner[:], fc2[:], start=True, stop=True).then_inc(fc2_done, 1)
                    rest(2)
                if back1:
                    pe.wait_ge(ln_hat[1], i)
                    if not ahead:
                        pe.wait_ge(x3_lo, i - 2)
                    transpose4(tr_b, hat).then_inc(x2_tr, 1)
                if cur:
                    pe.wait_ge(pt_lo, i + 1)
                    pe.wait_ge(pool_lo, POOL_LOS * (i + 1))
                    if ahead:
                        pe.wait_ge(u_lo, i + 2)
                    for j in range(2):
                        for hc in range(C):
                            for c in range(C):
                                mm = three(ua_ps[:, hc * P + j * L:hc * P + (j + 1) * L],
                                           both(ctx_nat[:, j], c, cols(hc)), both(probs_t, c, slice(j * L, (j + 1) * L)),
                                           c == 0, c == C - 1)
                    mm.then_inc(att_done, 1)
                    if straight and i == 0:
                        keep_clock(RESTS_FIRST[2])
                if back1:
                    pe.wait_ge(x2_lo, i)
                    after(pe, pos_done, i - 2)
                    if straight and i == 1:
                        pe.wait_ge(proj_lo, 3)
                    project(q_ps, W_Q, range(C)).then_inc(q_done, 1)
                if back1:
                    after(pe, masked_done, i - 1)
                    if straight and i == 1:
                        pe.wait_ge(proj_lo, 4)
                    project(k_ps, W_K, (0, 1))
                if back2:
                    pe.wait_ge(ln_hat[2], i - 1)
                    transpose4(tr_b, hat).then_inc(x3_tr, 1)
                    rest(3)
                if back1:
                    project(k_ps, W_K, (2, 3)).then_inc(k_done, 1)
                if back2:
                    pe.wait_ge(x3_lo, i - 1)
                    pe.wait_ge(q_cast, min(i, TILES) if straight else i)
                    for c in range(C):
                        mm = three(q_ps[:, RT:RT + E], both(x3_t, c, A), both(wg_split, c, A), c == 0, c == C - 1)
                    mm.then_inc(logits_mm, 1)
                    rest(4)
                if cur:
                    pe.wait_ge(att_lo, i + 1)
                    after(pe, x2_done, i - 1)
                    if straight and i == 0:
                        pe.wait_ge(proj_lo, 2)
                for c in range(C):
                    if cur:
                        mm = three(of_ps[:, :], both(att_t, c, A), both(W_O, c, A), c == 0, c == C - 1)
                    if ahead2 and c == 0:
                        pe.wait_ge(ln_hat[0], i + 3)
                        transpose4(tr_b, hat).then_inc(p_tr, 1)
                    if back2 and c == C - 2:
                        pe.wait_ge(onehot_done, i - 1)
                        pe.wait_ge(carry_done, i - 1)
                        pe.matmul(q_ps[:, PX:PX + E], before, onehot[:], start=True, stop=False)
                        pe.matmul(q_ps[:, PX:PX + E], ones16, carry[:], start=False, stop=True).then_inc(px_done, 1)
                        rest(5)
                if cur:
                    mm.then_inc(out_done, 1)

            pe.wait_ge(consts_in, 16)
            pe.wait_ge(ln_hat[0], 1)
            transpose4(tr_b, hat).then_inc(p_tr, 1)
            pe.wait_ge(p_hi, 1)
            keep_clock(RESTS_FIRST[0])
            each_step(pe, step)

            def transpose_rows(e):
                pe.wait_ge(e_norm, e + 1)
                transpose4(tr_a, e_hat).then_inc(e_tr, 1)
                if isinstance(e, int) and e == 0:
                    keep_clock(RESTS[1][6])

            def expert(e, k, p, turn):
                for kk, (which, hb) in enumerate(ORDER):
                    w = w_split[kk]
                    pe.wait_ge(w_lo[kk], e + 1)
                    if which == 1:
                        if kk == 0:
                            pe.wait_ge(e_lo, e + 1)
                        n = 4 * e + hb
                        after(pe, h_relu, n - 1)
                        for hc in range(C):
                            for c in range(C):
                                mm = three(hid_ps[hb % 2][:, cols(hc)], both(w, c, cols(hc)), both(e_t, c, A),
                                           c == 0, c == C - 1)
                        mm.then_inc(w_used, 1)
                    else:
                        pe.wait_ge(h_lo, 4 * e + hb + 1)
                        if hb == 0:
                            after(pe, y_out, e)
                            pe.wait_ge(e_sel, e + 1)
                            if turn == 0:
                                pe.wait_ge(b2_lo, 1)
                            pe.matmul(y_ps[:, :], sel, b2_split[:, 0], start=True, stop=False)
                            pe.matmul(y_ps[:, :], sel, b2_split[:, 1], start=False, stop=False)
                        for c in range(C):
                            mm = three(y_ps[:, :], both(hid_split[hb], cols(c)), both(w, c, A),
                                       False, hb == HB - 1 and c == C - 1)
                        mm.then_inc(w_used, 1)
                    if kk == 5 and turn < E - 1:
                        transpose_rows(e + 1)

            transpose_rows(0)
            each_expert(pe, expert)

        @block.scalar
        def _(act):
            def hi(dst, src, produced, count, done, scale=1.0):
                act.wait_ge(produced, count)
                act.activation(dst, src, ACT.Copy, scale=scale).then_inc(done, 1)

            def flat(a, s):
                return a[:, s].rearrange("p c n -> p (c n)")

            def proj_high(n):
                hi(proj[n][:, 0], proj_raw[n], proj_in[n], 16, proj_hi, scale=WS)

            def context_high(t, half):
                j, c = half // 2, 2 * (half % 2)
                if half % 2 == 0:
                    act.wait_ge(ctx_t_loaded[j], 16 * (t + 1))
                act.activation(ctx_t[:, j, 0, c:c + 2], ctx_t_raw[j][:, c:c + 2], ACT.Copy).then_inc(ctx_hi, 1)

            def natural_high(t, half):
                j, c = half // 2, 2 * (half % 2)
                if half % 2 == 0:
                    act.wait_ge(ctx_loaded[j], 16 * (t + 1))
                act.activation(ctx_nat[:, j, 0, c:c + 2], ctx_raw[j][:, c:c + 2], ACT.Copy).then_inc(nat_hi, 1)

            def normalise(n, t, source, moments):
                act.wait_ge(ln_shift[n], t + 1)
                act.activation(hat[:], source, ACT.Identity, bias=minus_mean[:, n:n + 1],
                               scale=moments[:, 1:2]).then_inc(ln_hat[n], 1)

            def step(i, k, p, ahead2, ahead, cur, back1, back2):
                straight = isinstance(i, int)
                if back2:
                    act.wait_ge(masked_done, i - 1)
                    after(act, h1_done, i - 2)
                    act.activation(exp_t[:], masked[:], ACT.Exp).then_inc(exp_done, 1)
                if ahead:
                    after(act, s_done, i + 1)
                    context_high(i + 1, 0)
                if cur:
                    act.wait_ge(s_shifted, i + 1)
                    after(act, pt_tr, i)
                    act.activation(probs[:], scores_ps[:, :], ACT.Exp, bias=s_shift, scale=1.0,
                                   accum_out=den).then_inc(p_exp, 1)
                if straight and i == -1:
                    for half in range(1, 4):
                        context_high(0, half)
                if ahead:
                    hi(flat(u_t, 0), ua_ps[:, :], u_done, i + 2, u_hi, scale=1.0 / WS)
                if back2:
                    act.wait_ge(h1_done, i - 1)
                    after(act, fc2_done, i - 2)
                    if straight and i == 2:
                        act.wait_ge(zeroed, 4)
                    act.activation(inner[:], small_ps[:, H1:H1 + P], ACT.Relu, bias=fc1_bias[:]).then_inc(inner_done, 1)
                if straight and i >= TILES:
                    chunk_high(0, LO_ON_POOL[0] if i == TILES else LO_ON_POOL[1])
                    if i > TILES:
                        chunk_high(0, LO_ON_DVE[2])
                if cur:
                    hi(flat(probs_t, 0), tr_a[:, :], pt_tr, i + 1, pt_hi)
                if straight and i == 1:
                    proj_high(3)
                if ahead and not (straight and i == -1):
                    context_high(i + 1, 1)
                if back1:
                    hi(flat(x2_t, 0), tr_b[:, :], x2_tr, i, x2_hi)
                if ahead and not (straight and i == -1):
                    context_high(i + 1, 2)
                    context_high(i + 1, 3)
                if cur:
                    if straight and i == 0:
                        proj_high(1)
                    hi(flat(att_t, 0), ua_ps[:, :], att_done, i + 1, att_hi)
                if ahead:
                    natural_high(i + 1, 0)
                if back2:
                    act.wait_ge(x2_tr, min(i, TILES) if straight else i)
                    if not (straight and i == TILES + 1):
                        normalise(2, i - 2, row[:, p, 0:D], row[:, p, D:D + 2])
                if back1:
                    after(act, roped, i - 1)
                    hi(qk[:, 0, :], q_ps[:, :], q_done, i, q_cast, scale=1.0 / WS)
                if back2:
                    hi(flat(x3_t, 0), tr_b[:, :], x3_tr, i - 1, x3_hi)
                if ahead:
                    natural_high(i + 1, 1)
                if ahead2:
                    if not back1:
                        act.wait_ge(p_tr, i + 2)
                    elif not back2:
                        act.wait_ge(x2_tr, i)
                    else:
                        act.wait_ge(x3_tr, i - 1)
                    normalise(0, i + 2, x_ahead[:], mv[:, 0])
                if back1:
                    hi(qk[:, 1, :], k_ps[:, :], k_done, i, k_cast, scale=1.0 / WS)
                if ahead2:
                    hi(flat(p_t, 0), tr_b[:, :], p_tr, i + 3, p_hi)
                if ahead:
                    natural_high(i + 1, 2)
                    natural_high(i + 1, 3)
                if back2:
                    act.wait_ge(l_negated, i - 1)
                    after(act, row_ready, i - 2)
                    act.activation(l_exp[:], logits[:], ACT.Exp, bias=l_neg, scale=1.0,
                                   accum_out=l_sum).then_inc(l_exped, 1)
                if straight and i == 0:
                    proj_high(2)
                    act.activation(wg_split[:, 0], wg_raw[:], ACT.Copy, scale=WS).then_inc(small_hi, 1)
                if straight and i == TILES - 1:
                    chunk_high(0, LO_ON_DVE[0])
                if straight and i == TILES:
                    chunk_high(0, LO_ON_DVE[1])
                if straight and i == TILES + 1:
                    for kk in LO_ON_DVE[3:]:
                        chunk_high(0, kk)

            normalise(0, 0, x_ahead[:], mv[:, 0])
            hi(flat(p_t, 0), tr_b[:, :], p_tr, 1, p_hi)
            proj_high(0)
            act.wait_ge(b_in, 16 * 2)
            act.activation(b_split[:, 0], b_raw[:], ACT.Copy, scale=WS).then_inc(small_hi, 1)

            def chunk_high(e, kk):
                if on_pool(e, kk):
                    act.wait_ge(w_scaled[kk], e + 1)
                else:
                    act.wait_ge(w_in[kk], 16 * (e + 1))
                after(act, w_used, CHUNKS * (e - 1) + kk + 1)
                act.activation(w_split[kk][:, 0], raw[kk], ACT.Copy,
                               scale=1.0 if on_pool(e, kk) else WS).then_inc(w_hi[kk], 1)

            each_step(act, step)

            def rows_hi(e):
                hi(flat(e_t, 0), tr_a[:, :], e_tr, e + 1, e_hi)

            def expert(e, k, p, turn):
                for kk, (which, hb) in enumerate(ORDER):
                    if which == 1:
                        act.wait_ge(w_used, CHUNKS * e + kk + 1)
                        after(act, h_lo, 4 * e + hb - 1)
                        if hb == 0:
                            act.wait_ge(b1_loaded[p], 16 * (k + 1))
                        for hc in range(C):
                            r = act.activation(hid[hb % 2][:, hc * P:(hc + 1) * P],
                                               hid_ps[hb % 2][:, hc * P:(hc + 1) * P], ACT.Relu,
                                               bias=b1_e[p][:, 4 * hb + hc:4 * hb + hc + 1], scale=1.0 / WS)
                        r.then_inc(h_relu, 1)
                    if kk == 6 and turn < E - 1:
                        rows_hi(e + 1)
                    if chunk_to_split(e, kk, turn):
                        chunk_high(*chunk_to_split(e, kk, turn))

            rows_hi(0)
            act.wait_ge(b2_in, 16)
            act.activation(b2_split[:, 0], b2_raw, ACT.Copy, scale=WS).then_inc(b2_hi, 1)
            each_expert(act, expert)

        @block.vector
        def _(dve):
            def lo(dst, src, high, done_hi, count, done, scale=1.0):
                dve.wait_ge(done_hi, count)
                if scale == 1.0:
                    dve.tensor_tensor(dst, src, high, ALU.subtract).then_inc(done, 1)
                else:
                    dve.scalar_tensor_tensor(out=dst, in0=src, scalar=scale, in1=high, op0=ALU.mult,
                                             op1=ALU.subtract).then_inc(done, 1)

            def flat(a, s):
                return a[:, s].rearrange("p c n -> p (c n)")

            def norm_stats(n, t, source, moments):
                dve.bn_stats(stats[:, n], source).then_inc(ln_stats[n], 1)
                alone(dve, ln_stats[n], t + 1)
                dve.bn_aggr(moments, stats[:, n]).then_inc(ln_mv[n], 1)

            dve.wait_ge(x_ahead_in, 16)
            norm_stats(0, 0, x_ahead[:], mv[:, 0])
            dve.memset(fc1_rows[:], 0.0).then_inc(zeroed, 1)
            dve.memset(fc1_bias[:], 0.0).then_inc(zeroed, 1)
            dve.memset(fc2[:], 0.0).then_inc(zeroed, 1)
            dve.memset(carry[:], 0.0).then_inc(carry_done, 1)
            dve.wait_ge(zeroed, 2)
            dve.memset(fc1_bias[32:33, :], 1.0).then_inc(zeroed, 1)
            dve.wait_ge(consts_in, 16)
            dve.tensor_copy(token[:], p_index).then_inc(token_next, 1)

            def proj_low(n):
                dve.wait_ge(proj_hi, n + 1)
                dve.scalar_tensor_tensor(out=proj[n][:, 1], in0=proj_raw[n], scalar=WS, in1=proj[n][:, 0],
                                         op0=ALU.mult, op1=ALU.subtract).then_inc(proj_lo, 1)

            def place(t, q):
                dve.wait_ge(l_exped, t + 1)
                dve.reciprocal(row[:, q, D + 2:D + 3], l_sum)
                dve.wait_ge(px_done, t + 1)
                dve.tensor_tensor_reduce(px_prod[:], q_ps[:, PX:PX + E], onehot[:], 1.0, 0.0,
                                         ALU.mult, ALU.add, pos).then_inc(pos_done, 1)
                dve.tensor_tensor(carry[:], carry[:], onehot[:], ALU.add).then_inc(carry_done, 1)
                dve.wait_ge(pos_done, t + 1)
                dve.tensor_scalar(over, pos, float(CAP), float(SKIP), ALU.is_ge, ALU.mult
                                  ).then_inc(over_done, 1)
                dve.wait_ge(base_done, t + 1)
                dve.tensor_tensor(slot_f[:], pos, base, ALU.add).then_inc(slot_f_done, 1)
                dve.wait_ge(slot_f_done, t + 1)
                dve.wait_ge(over_done, t + 1)
                dve.tensor_tensor(slot[:, q], slot_f[:], over, ALU.add).then_inc(row_ready, 1)

            def step(i, k, p, ahead2, ahead, cur, back1, back2):
                straight = isinstance(i, int)
                starting = straight and i == -1
                half = D // 2
                q = 1 - p

                def context_low(n):
                    if ahead:
                        j, c = n // 4, n % 4
                        lo(ctx_t[:, j, 1, c], ctx_t_raw[j][:, c], ctx_t[:, j, 0, c],
                           ctx_hi, 4 * (i + 1) + n // 2 + 1, ctx_lo)

                def stats_ahead():
                    dve.wait_ge(x_ahead_in, 16 * (i + 3))
                    norm_stats(0, i + 2, x_ahead[:], mv[:, 0])

                if starting:
                    lo(flat(p_t, 1), tr_b[:, :], flat(p_t, 0), p_hi, 1, p_lo)
                    proj_low(0)
                    dve.wait_ge(small_hi, 1)
                    dve.scalar_tensor_tensor(out=b_split[:, 1], in0=b_raw[:], scalar=WS, in1=b_split[:, 0],
                                             op0=ALU.mult, op1=ALU.subtract).then_inc(small_lo, 1)
                if back1:
                    dve.wait_ge(out_done, i)
                    if straight and i == 1:
                        dve.wait_ge(smalls_in, 16 * 3)
                    dve.wait_ge(rden_steps, 2 * i)
                    dve.scalar_tensor_tensor(out=x1[:, q], in0=of_ps[:, :], scalar=rden, in1=b_full[:],
                                             op0=ALU.mult, op1=ALU.add).then_inc(pre_done, 1)
                    dve.wait_ge(pre_done, i)
                    dve.wait_ge(x_res_in, 16 * i)
                    dve.scalar_tensor_tensor(out=x1[:, q], in0=x1[:, q], scalar=0.0, in1=x_res[:],
                                             op0=ALU.max, op1=ALU.add).then_inc(x1_done, 1)
                    dve.wait_ge(x1_done, i)
                    dve.bn_stats(stats[:, 1], x1[:, q]).then_inc(ln_stats[1], 1)
                if back2:
                    dve.wait_ge(st_done, i - 1)
                    after(dve, exp_done, i - 2)
                    dve.scalar_tensor_tensor(out=masked[:], in0=k_ps[:, 0:P], scalar=float(D) ** -0.5,
                                             in1=mask, op0=ALU.mult, op1=ALU.add).then_inc(masked_done, 1)
                if straight and i == TILES + 1:
                    chunk_low(0, LO_ON_DVE[1])
                if back1:
                    alone(dve, ln_stats[1], i)
                    dve.bn_aggr(mv[:, 1], stats[:, 1]).then_inc(ln_mv[1], 1)
                    dve.wait_ge(ln_mv[1], i)
                    rstd_guess(dve, 1, i - 1, mv[:, 1])
                if cur:
                    dve.wait_ge(s_done, i + 1)
                    dve.reduce_max(s_max, scores_ps[:, :], AX_X).then_inc(shift_steps, 1)
                    dve.wait_ge(shift_steps, 2 * i + 1)
                    dve.wait_ge(pb_done, i + 1)
                    dve.scalar_tensor_tensor(out=s_max_b, in0=small_ps[:, PB:PB + 1], scalar=1.0 / WS,
                                             in1=s_max, op0=ALU.mult, op1=ALU.add).then_inc(shift_steps, 1)
                    dve.wait_ge(shift_steps, 2 * i + 2)
                    dve.scalar_tensor_tensor(out=s_shift, in0=small_ps[:, PB:PB + 1], scalar=1.0 / WS,
                                             in1=s_max_b, op0=ALU.mult, op1=ALU.subtract).then_inc(s_shifted, 1)
                if back1:
                    rstd_newton(dve, 1, i - 1)
                    rstd_cubic(dve, 1, i - 1, mv[:, 1])
                    if ahead:
                        dve.wait_ge(p_tr, i + 2)
                    else:
                        dve.wait_ge(x3_tr, i - 2)
                    dve.wait_ge(ln_step[1], RSQRT_STEPS * i)
                    dve.tensor_scalar(hat[:], x1[:, q], mv[:, 1, 0:1], mv[:, 1, 1:2], ALU.subtract, ALU.mult
                                      ).then_inc(ln_hat[1], 1)
                if starting:
                    for n in range(CTX_ON_DVE):
                        context_low(n)
                    stats_ahead()
                if ahead:
                    lo(flat(u_t, 1), ua_ps[:, :], flat(u_t, 0), u_hi, i + 2, u_lo, scale=1.0 / WS)
                if cur:
                    dve.wait_ge(p_exp, i + 1)
                    dve.reciprocal(rden, den).then_inc(rden_steps, 1)
                    lo(flat(probs_t, 1), tr_a[:, :], flat(probs_t, 0), pt_hi, i + 1, pt_lo)
                    dve.wait_ge(rden_steps, 2 * i + 1)
                    dve.tensor_scalar(rden, rden, 1.0 / WS, None, ALU.mult).then_inc(rden_steps, 1)
                if back2:
                    dve.wait_ge(fc2_done, i - 1)
                    after(dve, scattered[p], 16 * (k - 1))
                    after(dve, base_out[p], 16 * (k - 1))
                    if straight and i == 3:
                        dve.wait_ge(filled, 16 * (E * CAP // P))
                    dve.tensor_tensor(row[:, p, 0:D], of_ps[:, :], x1[:, p], ALU.add).then_inc(x2_done, 1)
                    dve.wait_ge(x2_done, i - 1)
                    norm_stats(2, i - 2, row[:, p, 0:D], row[:, p, D:D + 2])
                if straight and i == TILES + 1:
                    dve.wait_ge(ln_mv[2], TILES)
                    rstd_guess(dve, 2, TILES - 1, row[:, p, D:D + 2])
                    rstd_newton(dve, 2, TILES - 1)
                    rstd_cubic(dve, 2, TILES - 1, row[:, p, D:D + 2])
                    dve.wait_ge(ln_step[2], RSQRT_STEPS * TILES)
                    dve.tensor_scalar(hat[:], row[:, p, 0:D], row[:, p, D:D + 1], row[:, p, D + 1:D + 2],
                                      ALU.subtract, ALU.mult).then_inc(ln_hat[2], 1)
                if back1:
                    lo(flat(x2_t, 1), tr_b[:, :], flat(x2_t, 0), x2_hi, i, x2_lo)
                if not straight or i >= 3:
                    place(i - 3, q)
                if straight and i == 1:
                    proj_low(3)
                if straight and i >= TILES:
                    chunk_low(0, LO_ON_DVE[0] if i == TILES else LO_ON_DVE[2])
                if not starting:
                    context_low(0)
                    context_low(1)
                if ahead2 and not starting:
                    stats_ahead()
                if straight and i == 0:
                    proj_low(1)
                if cur:
                    lo(flat(att_t, 1), ua_ps[:, :], flat(att_t, 0), att_hi, i + 1, att_lo)
                if not starting:
                    context_low(2)
                    context_low(3)
                    context_low(4)
                if back1:
                    dve.wait_ge(q_cast, i)
                    after(dve, st_done, i - 1)
                    dve.tensor_tensor(qk_rot[:, 0, 0:half], qk[:, 0, half:D], sin[:, 0:half], ALU.mult)
                    dve.tensor_tensor(qk_rot[:, 0, half:D], qk[:, 0, 0:half], sin[:, half:D], ALU.mult).then_inc(rope_sin, 1)
                if back2:
                    lo(flat(x3_t, 1), tr_b[:, :], flat(x3_t, 0), x3_hi, i - 1, x3_lo)
                if not starting:
                    context_low(5)
                if back1:
                    dve.wait_ge(rope_sin, 2 * i - 1)
                    dve.tensor_tensor(qk[:, 0], qk[:, 0], cos, ALU.mult)
                if back2:
                    dve.wait_ge(logits_mm, i - 1)
                    dve.scalar_tensor_tensor(out=logits[:], in0=q_ps[:, RT:RT + E], scalar=1.0 / WS,
                                             in1=bg_full[:], op0=ALU.mult, op1=ALU.add).then_inc(logits_done, 1)
                    dve.wait_ge(logits_done, i - 1)
                    dve.reduce_max(l_max, logits[:], AX_X).then_inc(l_maxed, 1)
                    dve.wait_ge(token_next, i - 1)
                    dve.tensor_copy(row[:, p, D + 3:D + 4].bitcast(I32), token[:]).then_inc(token_written, 1)
                    dve.wait_ge(l_maxed, i - 1)
                    dve.scalar_tensor_tensor(out=cand[:], in0=logits[:], scalar=l_max, in1=desc,
                                             op0=ALU.is_equal, op1=ALU.mult).then_inc(cand_done, 1)
                    dve.tensor_scalar(l_neg, l_max, -1.0, None, ALU.mult).then_inc(l_negated, 1)
                    dve.wait_ge(cand_done, i - 1)
                    dve.reduce_max(rank, cand[:], AX_X).then_inc(rank_done, 1)
                    dve.wait_ge(token_written, i - 1)
                    dve.tensor_scalar(token[:], token[:], float(P), None, ALU.add).then_inc(token_next, 1)
                    dve.wait_ge(rank_done, i - 1)
                    dve.tensor_scalar(onehot[:], desc, rank, None, ALU.is_equal).then_inc(onehot_done, 1)
                    dve.tensor_scalar(base, rank, -float(CAP), float(E * CAP), ALU.mult, ALU.add
                                      ).then_inc(base_done, 1)
                if back1:
                    dve.wait_ge(k_cast, i)
                    dve.tensor_tensor(qk_rot[:, 1, 0:half], qk[:, 1, half:D], sin[:, 0:half], ALU.mult)
                    dve.tensor_tensor(qk_rot[:, 1, half:D], qk[:, 1, 0:half], sin[:, half:D], ALU.mult).then_inc(rope_sin, 1)
                    dve.wait_ge(rope_sin, 2 * i)
                    dve.tensor_tensor(qk[:, 1], qk[:, 1], cos, ALU.mult).then_inc(rope_cos, 1)
                if ahead2:
                    lo(flat(p_t, 1), tr_b[:, :], flat(p_t, 0), p_hi, i + 3, p_lo)
                if back1:
                    dve.wait_ge(rope_cos, i)
                    dve.tensor_tensor(qk_rot[:, :, :], qk[:, :, :], qk_rot[:, :, :], ALU.add).then_inc(roped, 1)
                if straight and i == TILES + 1:
                    place(i - 2, p)
                    dve.wait_ge(k_done, TILES)
                    dve.memset(b2_raw, 0.0).then_inc(b2_zero, 1)
                    dve.memset(e_index, 0.0).then_inc(e_idx, 1)
                    for kk in LO_ON_DVE[3:]:
                        chunk_low(0, kk)
                if straight and i == 0:
                    proj_low(2)
                    dve.wait_ge(small_hi, 2)
                    dve.scalar_tensor_tensor(out=wg_split[:, 1], in0=wg_raw[:], scalar=WS, in1=wg_split[:, 0],
                                             op0=ALU.mult, op1=ALU.subtract).then_inc(small_lo, 1)

            def chunk_low(e, kk):
                if not on_pool(e, kk):
                    w = w_split[kk]
                    lo(w[:, 1], raw[kk], w[:, 0], w_hi[kk], e + 1, w_lo[kk], scale=WS)

            each_step(dve, step)

            def rows_hat(e, k, p):
                dve.wait_ge(e_loaded[p], 16 * (k + 1))
                after(dve, e_tr, e)
                dve.tensor_scalar(e_hat, e_row[p][:, 0:D], e_row[p][:, D:D + 1], e_row[p][:, D + 1:D + 2],
                                  ALU.subtract, ALU.mult).then_inc(e_norm, 1)
                dve.tensor_copy(e_x[p], e_row[p][:, 0:D])
                dve.tensor_copy(token_next_e[p], e_row[p][:, D + 3:D + 4].bitcast(U32))
                dve.tensor_scalar(gate_e[p], e_row[p][:, D + 2:D + 3], 1.0 / WS, None, ALU.mult).then_inc(gate_done, 1)

            def rows_lo(e):
                lo(flat(e_t, 1), tr_a[:, :], flat(e_t, 0), e_hi, e + 1, e_lo)
                dve.wait_ge(e_idx, e + 1)
                dve.tensor_scalar(is_e, p_index, e_index[:, 0:1], None, ALU.is_equal).then_inc(e_sel_steps, 1)
                dve.wait_ge(e_sel_steps, e + 1)
                dve.tensor_scalar(sel, ones16, is_e[:, 0:1], None, ALU.mult).then_inc(e_sel, 1)
                dve.tensor_scalar(e_index, e_index, 1.0, None, ALU.add).then_inc(e_idx, 1)

            def expert(e, k, p, turn):
                kn, pn = neighbour(k, p, 1)
                for kk, (which, hb) in enumerate(ORDER):
                    if kk == 3 and turn < E - 1:
                        rows_hat(e + 1, kn, pn)
                    if which == 1:
                        n = 4 * e + hb
                        dve.wait_ge(h_relu, n + 1)
                        dve.tensor_copy(hid_split[hb][:, 0], hid[hb % 2]).then_inc(h_hi, 1)
                        lo(hid_split[hb][:, 1], hid[hb % 2], hid_split[hb][:, 0], h_hi, n + 1, h_lo)
                    if kk == CHUNKS - 1:
                        dve.wait_ge(w_used, CHUNKS * (e + 1))
                        dve.wait_ge(gate_done, e + 1)
                        after(dve, out_scat[p], 16 * k)
                        dve.tensor_copy(token_e[p], token_next_e[p])
                        dve.scalar_tensor_tensor(out=o_row[p], in0=y_ps[:, :], scalar=gate_e[p][:, 0:1],
                                                 in1=e_x[p], op0=ALU.mult, op1=ALU.add).then_inc(y_out, 1)
                    if kk == 6 and turn < E - 1:
                        rows_lo(e + 1)
                    if chunk_to_split(e, kk, turn):
                        chunk_low(*chunk_to_split(e, kk, turn))

            rows_hat(0, 0, 0)
            rows_lo(0)
            dve.wait_ge(b2_hi, 1)
            dve.scalar_tensor_tensor(out=b2_split[:, 1], in0=b2_raw, scalar=WS, in1=b2_split[:, 0],
                                     op0=ALU.mult, op1=ALU.subtract).then_inc(b2_lo, 1)
            each_expert(dve, expert)

        @block.gpsimd
        def _(pool):
            pool.memset(fill[:, 0:D + 3], 0.0).then_inc(begun, 1)
            pool.memset(fill[:, D + 3:D + 4].bitcast(I32), SKIP).then_inc(begun, 1)

            def rstd(n, t, moments):
                alone(pool, ln_mv[n], t + 1)
                rstd_guess(pool, n, t, moments)
                rstd_newton(pool, n, t)
                rstd_cubic(pool, n, t, moments)
                alone(pool, ln_step[n], RSQRT_STEPS * (t + 1))
                pool.tensor_scalar(minus_mean[:, n:n + 1], moments[:, 0:1], moments[:, 1:2], -1.0, ALU.mult, ALU.mult
                                   ).then_inc(ln_shift[n], 1)

            rstd(0, 0, mv[:, 0])

            def step(i, k, p, ahead2, ahead, cur, back1, back2):
                if back2 and not (isinstance(i, int) and i == TILES + 1):
                    rstd(2, i - 2, row[:, p, D:D + 2])
                if ahead2 and not (isinstance(i, int) and i == -1):
                    rstd(0, i + 2, mv[:, 0])
                if ahead:
                    for c in range(CTX_ON_DVE - C, C):
                        alone(pool, ctx_hi, 4 * (i + 1) + 4)
                        pool.tensor_tensor(ctx_t[:, 1, 1, c], ctx_t_raw[1][:, c], ctx_t[:, 1, 0, c], ALU.subtract
                                           ).then_inc(pool_lo, 1)
                    if isinstance(i, int) and i == -1:
                        rstd(0, i + 2, mv[:, 0])
                if isinstance(i, int) and i == TILES + 1:
                    pool.wait_ge(x2_done, TILES)
                if back2:
                    pool.dma_start(out[bass.ds((i - 2) * P, P), :], row[:, p, 0:D]).then_inc(base_out[p], 16)
                if not isinstance(i, int) or i >= 3:
                    scatter_row(i - 3, *neighbour(k, p, -3))
                if ahead:
                    for j in range(2):
                        alone(pool, nat_hi, 4 * (i + 1) + 2 * j + 2)
                        pool.tensor_tensor(ctx_nat[:, j, 1], ctx_raw[j], ctx_nat[:, j, 0], ALU.subtract
                                           ).then_inc(pool_lo, 1)
                if isinstance(i, int) and i == TILES - 1:
                    scale_chunk(0, LO_ON_POOL[0])
                if isinstance(i, int) and i == TILES:
                    low_and_scale(0, LO_ON_POOL[0])
                if isinstance(i, int) and i == TILES + 1:
                    scatter_row(i - 2, k - 1, p)

            def scatter_row(t, kt, q):
                alone(pool, row_ready, t + 1)
                alone(pool, ln_step[2], RSQRT_STEPS * (t + 1))
                if isinstance(t, int) and t == 0:
                    pool.wait_ge(filled, 16 * (E * CAP // P))
                alone(pool, scattered[1 - q], 16 * (neighbour(kt, q, -1)[0] + 1))
                pool.indirect_dma_start(
                    out=slot_table, out_offset=bass.IndirectOffsetOnAxis(ap=slot[:, q].bitcast(U32), axis=0),
                    in_=row[:, q, :], in_offset=None, bounds_check=E * CAP - 1, oob_is_err=False,
                ).then_inc(scattered[q], 16)

            def scale_chunk(e, kk):
                alone(pool, w_in[kk], 16 * (e + 1))
                pool.tensor_scalar(raw[kk], raw[kk], WS, 1.0, ALU.mult, ALU.mult).then_inc(w_scaled[kk], 1)

            def chunk_low(e, kk):
                w = w_split[kk]
                alone(pool, w_hi[kk], e + 1)
                pool.tensor_tensor(w[:, 1], raw[kk], w[:, 0], ALU.subtract).then_inc(w_lo[kk], 1)

            def low_and_scale(e, kk):
                chunk_low(e, kk)
                m = LO_ON_POOL.index(kk) + 1
                e, kk = (e, LO_ON_POOL[m]) if m < len(LO_ON_POOL) else (e + 1, LO_ON_POOL[0])
                if on_pool(e, kk):
                    scale_chunk(e, kk)

            each_step(pool, step)

            def scatter_out(e, k, p):
                alone(pool, y_out, e + 1)
                alone(pool, out_scat[1 - p], 16 * (neighbour(k, p, -1)[0] + 1))
                pool.indirect_dma_start(
                    out=out, out_offset=bass.IndirectOffsetOnAxis(ap=token_e[p], axis=0),
                    in_=o_row[p], in_offset=None, bounds_check=TOK - 1, oob_is_err=False,
                ).then_inc(out_scat[p], 16)

            def expert(e, k, p, turn):
                kb, pb = neighbour(k, p, -1)
                for kk in range(CHUNKS):
                    if kk == 0 and not (isinstance(e, int) and e == 0):
                        scatter_out(e - 1, kb, pb)
                    if chunk_to_split(e, kk, turn) and on_pool(*chunk_to_split(e, kk, turn)):
                        low_and_scale(*chunk_to_split(e, kk, turn))

            low_and_scale(0, LO_ON_POOL[1])
            for n in range(2):
                pool.wait_ge(base_out[n], 16 * (TILES // 2))
            each_expert(pool, expert)
            scatter_out(E - 1, E // 2 - 1, 1)
            for n in range(2):
                pool.wait_ge(out_scat[n], 16 * (E // 2))


def tables():
    k, q = np.arange(P)[:, None], np.arange(P)[None, :]
    mask = np.where((k // L == q // L) & (k <= q), 0.0, NEG).astype(np.float32)
    desc = np.broadcast_to(E - np.arange(E, dtype=np.float32), (P, E))
    f32 = np.concatenate([np.eye(P, dtype=np.float32), mask, desc, np.arange(P, dtype=np.float32)[:, None]], 1)
    inv = (np.float32(ROPE_BASE) ** (-np.arange(0, D, 2, dtype=np.float32) / np.float32(D))).astype(np.float32)
    angle = np.arange(L, dtype=np.float32)[None, :] * inv[:, None]
    parts = []
    for f, sign in ((np.cos, (1, 1)), (np.sin, (-1, 1))):
        v = f(angle).astype(np.float32).reshape(C // 2, P, L).transpose(1, 0, 2)
        v = np.concatenate([sign[0] * v, sign[1] * v], 1)
        parts.append(np.concatenate([v, v], 2).reshape(P, D))
    parts += [(k < q).astype(np.float32), np.ones((P, P), np.float32)]
    return np.ascontiguousarray(f32), np.concatenate(parts, 1)


def kernel(**inputs):
    import ml_dtypes
    from concourse import bacc
    from concourse.bass_utils import run_bass_kernel_spmd

    def a(name):
        return np.asarray(inputs[name])

    f32, f16 = tables()
    w = a("L0_xattn_W")
    ctx = a("ctx_1024")
    arrays = {
        "x": a("x").reshape(TOK, D),
        "ctx": ctx,
        "ctx_tr": ctx.reshape(B, P, 4, C, P).transpose(0, 4, 3, 2, 1).reshape(B, P, C, LQ),
        "w_nat": w,
        "w_t": w.T,
        "wq_t": a("L0_attn_Wq").T,
        "wk_t": a("L0_attn_Wk").T,
        "b_row": a("L0_xattn_b"),
        "b_col": a("L0_xattn_b").reshape(C, P).T,
        "fc1_w": a("L0_attn_fc1_w").reshape(INNER),
        "fc1_b": a("L0_attn_fc1_b").reshape(INNER, 1),
        "fc2_t": a("L0_attn_fc2_w").T,
        "fc2_b": a("L0_attn_fc2_b").reshape(1, D),
        "wg": a("L0_ffn_Wg"),
        "bg": a("L0_ffn_bg"),
        "w1": a("L0_ffn_W1").reshape(E, C, P, HB, D).transpose(0, 3, 2, 1, 4),
        "b1": a("L0_ffn_b1").reshape(E, H // P, P).transpose(0, 2, 1),
        "w2": a("L0_ffn_W2").reshape(E, HB, C, P, D).transpose(0, 1, 3, 2, 4),
        "b2": a("L0_ffn_b2"),
        "consts": f32,
        "consts16": f16.astype(ml_dtypes.bfloat16),
    }
    arrays = {n: np.ascontiguousarray(v) for n, v in arrays.items()}
    nc = bacc.Bacc("TRN2", target_bir_lowering=False, num_devices=1)
    args = {n: nc.dram_tensor(n, v.shape, mybir.dt.from_np(v.dtype), kind="ExternalInput").ap()
            for n, v in arrays.items()}
    out = nc.dram_tensor("out", [TOK, D], F32, kind="ExternalOutput").ap()
    program(nc, out=out, **args)
    r = run_bass_kernel_spmd(nc, [arrays], core_ids=[0])
    return r.results[0]["out"].reshape(B, L, D)
```
